# Optimizing a Trainium2 kernel written in Bass

```python
import numpy as np
import jax
import jax.numpy as jnp

def _softmax(x, axis=-1):
    return jax.nn.softmax(x, axis=axis)

def _gelu(x):
    return jax.nn.gelu(x, approximate=True)

def _silu(x):
    return jax.nn.silu(x)

def _sigmoid(x):
    return jax.nn.sigmoid(x)

def _layernorm(x, axis=-1, eps=1e-05):
    m = jnp.mean(x, axis=axis, keepdims=True)
    v = jnp.var(x, axis=axis, keepdims=True)
    return (x - m) / jnp.sqrt(v + eps)

def _scatter_add(tgt, idx, src, axis=0):
    return tgt.at[idx].add(src)

def _segment_sum(src, seg, n):
    return jax.ops.segment_sum(src, seg, n)
kernel_name = 'mk_early_fusion_d1_tok_img1024_r4_cbb99f'

def setup_inputs(seed: int=0):
    np.random.seed(seed)
    _w = jnp.asarray

    def _rec_inputs():
        import jax
        import jax.numpy as jnp
        _rk = jax.random.key(seed)
        x = -0.00016672 + 0.999947 * jax.random.normal(jax.random.fold_in(_rk, 1), (8, 3, 128, 128), jnp.float32)
        txt = -6.7295e-12 + 0.999995 * jax.random.normal(jax.random.fold_in(_rk, 2), (8, 128, 256), jnp.float32)
        return (x, txt)
    x, txt = _rec_inputs()

    def _L0_tok_setup():
        import jax, jax.numpy as jnp
        import numpy as np
        EPS = 1e-05
        PH = PW = 16

        def _layernorm(x, g, b):
            mu = jnp.mean(x, axis=-1, keepdims=True)
            var = jnp.mean(jnp.square(x - mu), axis=-1, keepdims=True)
            return (x - mu) * jax.lax.rsqrt(var + EPS) * g + b
        key = jax.random.key(seed)
        k1, k2 = jax.random.split(key)
        B, C, H, W_ = (64, 3, 96, 96)
        patch_dim, input_dim = (C * PH * PW, 256)
        img = jax.random.normal(k1, (B, C, H, W_), dtype=jnp.float32)
        W = jax.random.normal(k2, (patch_dim, input_dim), dtype=jnp.float32) * patch_dim ** (-0.5)
        return {'img': img, 'ln1_g': jnp.ones((patch_dim,), jnp.float32), 'ln1_b': jnp.zeros((patch_dim,), jnp.float32), 'W': W, 'b': jnp.zeros((input_dim,), jnp.float32), 'ln2_g': jnp.ones((input_dim,), jnp.float32), 'ln2_b': jnp.zeros((input_dim,), jnp.float32)}
    _L0_tok_all = _L0_tok_setup()
    _L0_tok_in = {k: v for k, v in _L0_tok_all.items() if k in ('ln1_g', 'ln1_b', 'W', 'b', 'ln2_g', 'ln2_b')}
    del _L0_tok_all

    def _L0_attn_setup():
        import jax, jax.numpy as jnp
        import numpy as np
        import math
        B, N, DIM, H, DH, NNULL = (2, 512, 256, 16, 64, 2)
        SCALE = 8.0
        LN_EPS = 1e-05

        def _alibi_slopes(heads):
            start = 2.0 ** (-2.0 ** (-(math.log2(heads) - 3)))
            return np.array([start * start ** i for i in range(heads)], dtype=np.float32)

        def _l2norm(t):
            n = jnp.sqrt(jnp.sum(t * t, axis=-1, keepdims=True))
            return t / jnp.maximum(n, 1e-12)
        key = jax.random.key(seed)
        ks = jax.random.split(key, 6)
        inner = H * DH
        return {'x': jax.random.normal(ks[0], (B, N, DIM), dtype=jnp.float32), 'norm_g': jnp.ones((DIM,), jnp.float32), 'norm_b': jnp.zeros((DIM,), jnp.float32), 'Wq': jax.random.normal(ks[1], (DIM, inner), jnp.float32) * 0.02, 'Wkv': jax.random.normal(ks[2], (DIM, 2 * inner), jnp.float32) * 0.02, 'q_scale': jnp.ones((DH,), jnp.float32), 'k_scale': jnp.ones((DH,), jnp.float32), 'null_kv': jax.random.normal(ks[3], (H, 2 * NNULL, DH), jnp.float32), 'Wout': jax.random.normal(ks[4], (inner, DIM), jnp.float32) * 0.02}
    _L0_attn_all = _L0_attn_setup()
    _L0_attn_in = {k: v for k, v in _L0_attn_all.items() if k in ('norm_g', 'norm_b', 'Wq', 'Wkv', 'q_scale', 'k_scale', 'null_kv', 'Wout')}
    del _L0_attn_all

    def _L0_ffn_setup():
        import jax, jax.numpy as jnp
        import numpy as np
        B, T, H = (2, 512, 256)
        I = 1024
        HEADS = 4
        RET = 128
        NUM_EXPERTS = 1024
        NUM_KEYS = 64
        K = 8
        key = jax.random.key(seed)
        ks = jax.random.split(key, 7)
        return {'hidden_states': jax.random.normal(ks[0], (B, T, H), jnp.float32), 'W_up': jax.random.normal(ks[1], (I, H), jnp.float32) * 0.02, 'W_down': jax.random.normal(ks[2], (H, I), jnp.float32) * 0.02, 'W_q': jax.random.normal(ks[3], (HEADS * RET, H), jnp.float32) * 0.02, 'keys': jax.random.normal(ks[4], (HEADS, NUM_KEYS, 2, RET // 2), jnp.float32) * 0.02, 'down_embed': jax.random.normal(ks[5], (NUM_EXPERTS, H), jnp.float32) * 0.02, 'up_embed': jax.random.normal(ks[6], (NUM_EXPERTS, H), jnp.float32) * 0.02}
    _L0_ffn_all = _L0_ffn_setup()
    _L0_ffn_in = {k: v for k, v in _L0_ffn_all.items() if k in ('W_up', 'W_down', 'W_q', 'keys', 'down_embed', 'up_embed')}
    del _L0_ffn_all
    return {'x': x, 'txt': txt, 'L0_tok_ln1_g': _L0_tok_in['ln1_g'], 'L0_tok_ln1_b': _L0_tok_in['ln1_b'], 'L0_tok_W': _L0_tok_in['W'], 'L0_tok_b': _L0_tok_in['b'], 'L0_tok_ln2_g': _L0_tok_in['ln2_g'], 'L0_tok_ln2_b': _L0_tok_in['ln2_b'], 'L0_attn_norm_g': _L0_attn_in['norm_g'], 'L0_attn_norm_b': _L0_attn_in['norm_b'], 'L0_attn_Wq': _L0_attn_in['Wq'], 'L0_attn_Wkv': _L0_attn_in['Wkv'], 'L0_attn_q_scale': _L0_attn_in['q_scale'], 'L0_attn_k_scale': _L0_attn_in['k_scale'], 'L0_attn_null_kv': _L0_attn_in['null_kv'], 'L0_attn_Wout': _L0_attn_in['Wout'], 'L0_ffn_W_up': _L0_ffn_in['W_up'], 'L0_ffn_W_down': _L0_ffn_in['W_down'], 'L0_ffn_W_q': _L0_ffn_in['W_q'], 'L0_ffn_keys': _L0_ffn_in['keys'], 'L0_ffn_down_embed': _L0_ffn_in['down_embed'], 'L0_ffn_up_embed': _L0_ffn_in['up_embed']}

def reference(x, txt, L0_tok_ln1_g, L0_tok_ln1_b, L0_tok_W, L0_tok_b, L0_tok_ln2_g, L0_tok_ln2_b, L0_attn_norm_g, L0_attn_norm_b, L0_attn_Wq, L0_attn_Wkv, L0_attn_q_scale, L0_attn_k_scale, L0_attn_null_kv, L0_attn_Wout, L0_ffn_W_up, L0_ffn_W_down, L0_ffn_W_q, L0_ffn_keys, L0_ffn_down_embed, L0_ffn_up_embed):
    import jax
    import jax.numpy as jnp

    def _L0_tok_ref(img, ln1_g, ln1_b, W, b, ln2_g, ln2_b):
        import jax, jax.numpy as jnp
        import numpy as np
        EPS = 1e-05
        PH = PW = 16

        def _layernorm(x, g, b):
            mu = jnp.mean(x, axis=-1, keepdims=True)
            var = jnp.mean(jnp.square(x - mu), axis=-1, keepdims=True)
            return (x - mu) * jax.lax.rsqrt(var + EPS) * g + b
        B, C, H, Wd = img.shape
        x = img.reshape(B, C, H // PH, PH, Wd // PW, PW)
        x = jnp.transpose(x, (0, 2, 4, 3, 5, 1))
        x = x.reshape(B, -1, PH * PW * C)
        x = _layernorm(x, ln1_g, ln1_b)
        x = jnp.einsum('bnd,de->bne', x, W) + b
        x = _layernorm(x, ln2_g, ln2_b)
        return x

    def _L0_attn_ref(x, norm_g, norm_b, Wq, Wkv, q_scale, k_scale, null_kv, Wout):
        import jax, jax.numpy as jnp
        import numpy as np
        import math
        B, N, DIM, H, DH, NNULL = (2, 512, 256, 16, 64, 2)
        SCALE = 8.0
        LN_EPS = 1e-05

        def _alibi_slopes(heads):
            start = 2.0 ** (-2.0 ** (-(math.log2(heads) - 3)))
            return np.array([start * start ** i for i in range(heads)], dtype=np.float32)

        def _l2norm(t):
            n = jnp.sqrt(jnp.sum(t * t, axis=-1, keepdims=True))
            return t / jnp.maximum(n, 1e-12)
        b, n, dim = x.shape
        h, dh, nn = (H, DH, NNULL)
        j = n + nn
        mu = jnp.mean(x, axis=-1, keepdims=True)
        var = jnp.mean((x - mu) ** 2, axis=-1, keepdims=True)
        xn = (x - mu) * jax.lax.rsqrt(var + LN_EPS) * norm_g + norm_b
        q = (xn @ Wq).reshape(b, n, h, dh).transpose(0, 2, 1, 3)
        kv = x @ Wkv
        k, v = jnp.split(kv, 2, axis=-1)
        k = k.reshape(b, n, h, dh).transpose(0, 2, 1, 3)
        v = v.reshape(b, n, h, dh).transpose(0, 2, 1, 3)
        null = null_kv.reshape(h, nn, 2, dh)
        nk = jnp.broadcast_to(null[:, :, 0, :][None], (b, h, nn, dh))
        nv = jnp.broadcast_to(null[:, :, 1, :][None], (b, h, nn, dh))
        k = jnp.concatenate([nk, k], axis=2)
        v = jnp.concatenate([nv, v], axis=2)
        q = _l2norm(q) * q_scale
        k = _l2norm(k) * k_scale
        sim = jnp.einsum('bhid,bhjd->bhij', q, k) * SCALE
        irow = jnp.arange(j - n, j)
        jcol = jnp.arange(j)
        bias = -jnp.abs(jcol[None, :] - irow[:, None]).astype(sim.dtype)
        slopes = jnp.asarray(_alibi_slopes(h))[:, None, None]
        sim = sim + slopes * bias
        causal = jnp.triu(jnp.ones((n, j), dtype=bool), k=j - n + 1)
        neg = jnp.finfo(sim.dtype).max
        sim = jnp.where(causal[None, None], -neg, sim)
        attn = jax.nn.softmax(sim, axis=-1)
        out = jnp.einsum('bhij,bhjd->bhid', attn, v)
        out = out.transpose(0, 2, 1, 3).reshape(b, n, h * dh)
        return out @ Wout

    def _L0_ffn_ref(hidden_states, W_up, W_down, W_q, keys, down_embed, up_embed):
        import jax, jax.numpy as jnp
        import numpy as np
        B, T, H = (2, 512, 256)
        I = 1024
        HEADS = 4
        RET = 128
        NUM_EXPERTS = 1024
        NUM_KEYS = 64
        K = 8
        b, t, hd = hidden_states.shape
        h, nk, _, n = keys.shape
        q = jnp.einsum('btd,ed->bte', hidden_states, W_q)
        q = q.reshape(b, t, 2, h, n).transpose(2, 0, 1, 3, 4)
        sim = jnp.einsum('pbthn,hkpn->pbthk', q, keys)
        scores_xy, idx_xy = jax.lax.top_k(sim, K)
        sx, sy = (scores_xy[0], scores_xy[1])
        ix, iy = (idx_xy[0], idx_xy[1])
        all_scores = (sx[..., :, None] + sy[..., None, :]).reshape(b, t, h, K * K)
        all_idx = (ix[..., :, None] * nk + iy[..., None, :]).reshape(b, t, h, K * K)
        scores, pk = jax.lax.top_k(all_scores, K)
        indices = jnp.take_along_axis(all_idx, pk, axis=-1)
        de = down_embed[indices]
        ue = up_embed[indices]
        w = jax.nn.silu(jnp.einsum('btd,bthkd->bthk', hidden_states, de) * jax.nn.softmax(scores, axis=-1))
        experts_states = jnp.einsum('bthk,bthkd->btd', w, ue)
        dense = jnp.einsum('bti,di->btd', jax.nn.silu(jnp.einsum('btd,id->bti', hidden_states, W_up)), W_down)
        return dense + experts_states
    h = _L0_tok_ref(x, L0_tok_ln1_g, L0_tok_ln1_b, L0_tok_W, L0_tok_b, L0_tok_ln2_g, L0_tok_ln2_b)
    h = jnp.concatenate([h, txt], axis=1)
    h = h + _L0_attn_ref(_layernorm(h, axis=-1), L0_attn_norm_g, L0_attn_norm_b, L0_attn_Wq, L0_attn_Wkv, L0_attn_q_scale, L0_attn_k_scale, L0_attn_null_kv, L0_attn_Wout)
    h = h + _L0_ffn_ref(_layernorm(h, axis=-1), L0_ffn_W_up, L0_ffn_W_down, L0_ffn_W_q, L0_ffn_keys, L0_ffn_down_embed, L0_ffn_up_embed)
    return h

_drawn_inputs = setup_inputs


def setup_inputs(seed=0):
    import zlib

    import numpy as np

    out = dict(_drawn_inputs(seed))
    spreads = {'L0_tok_ln1_g': (1.0, 0.2),
     'L0_tok_ln1_b': (0.0, 0.1),
     'L0_tok_b': (0.0, 0.1),
     'L0_tok_ln2_g': (1.0, 0.2),
     'L0_tok_ln2_b': (0.0, 0.1),
     'L0_attn_norm_g': (1.0, 0.6),
     'L0_attn_norm_b': (0.0, 0.8),
     'L0_attn_q_scale': (1.0, 0.6),
     'L0_attn_k_scale': (1.0, 0.6)}
    factors = {'L0_ffn_W_q': 8.0,
     'L0_ffn_keys': 8.0,
     'L0_ffn_down_embed': 5.427,
     'L0_ffn_up_embed': 5.743}
    for name, (base, spread) in spreads.items():
        noise = np.random.default_rng([zlib.crc32(name.encode()), seed]).standard_normal(out[name].shape)
        drawn = base * np.exp(spread * noise) if base else spread * noise
        out[name] = jnp.asarray(drawn.astype(out[name].dtype))
    for name, factor in factors.items():
        out[name] = (out[name] * factor).astype(out[name].dtype)
    return out
```

```python
from contextlib import ExitStack

import concourse.bass as bass
from concourse import mybir

B, TXT, DIM = 8, 128, 256
GRID, PATCH, CH = 8, 16, 3
NPATCH = GRID * GRID
PDIM = CH * PATCH * PATCH
N = NPATCH + TXT
P = 128
TILES = B * N // P
GROUPS = 4
TPG = TILES // GROUPS
TOK = TPG * P
HEADS, DH, NULL = 16, 64, 2
PAIRS = HEADS // 2
INNER = HEADS * DH
QB = N // 2
KA = QB + NULL
KEYS = N + NULL
SC = KA + KEYS
VAT = 3 * QB
DC = DIM // P
PC = PDIM // P
FF = 1024
FC = FF // P
RH, RN, NKEY, TOPK = 4, 64, 64, 8
EXPERTS = 1024
EX = EXPERTS // NKEY
EC = EXPERTS // P
SEL_LEN = 37
EPS = 1e-5
BIG = 3.0e38


def build_program(nc, patches, txt, ln1_g, ln1_b, tokW, tok_b, ln2_g, ln2_b, norm_g, norm_b, Wq, Wkv,
                  q_scale, k_scale, null_k, null_v, Wout, WupT, WdownT, WrT, keysT, downT, upE, out):
    fp32, fp16, u32 = mybir.dt.float32, mybir.dt.float16, mybir.dt.uint32
    ALU = mybir.AluOpType
    ACT = mybir.ActivationFunctionType
    AX = mybir.AxisListType

    ctx = ExitStack()
    with ctx:
        phase = ExitStack()

        def sb(name, shape, dt=fp32):
            return ctx.enter_context(nc.sbuf_tensor(name, shape, dt))

        def tmp(name, shape, dt=fp32):
            return phase.enter_context(nc.sbuf_tensor(name, shape, dt))

        def sem(name):
            return ctx.enter_context(nc.semaphore(name))

        ln1g_sb = sb("ln1g_sb", [P, PC])
        ln1b_sb = sb("ln1b_sb", [P, PC])
        rows_sb = sb("rows_sb", [P, 3, DIM])
        ng_sb = sb("ng_sb", [P, DC])
        nb_sb = sb("nb_sb", [P, DC])
        Wup_sb = sb("Wup_sb", [P, DC, FF])
        Wdn_sb = sb("Wdn_sb", [P, FC, DIM])
        Wr_sb = sb("Wr_sb", [P, DC, 2 * RH * RN])
        Wout_sb = sb("Wout_sb", [P, PAIRS, DIM])
        keyB = sb("keyB", [P, RH, P])
        down_sb = sb("down_sb", [P, DC, EXPERTS])
        up_sb = sb("up_sb", [P, EC, DIM])
        ident = sb("ident", [P, P])
        qk_raw = sb("qk_raw", [P, 2])
        qks = sb("qks", [P, 1])
        half = sb("half", [P, 16])
        nullk = sb("nullk", [2 * PAIRS, 2, DH])
        nullk_sq = sb("nullk_sq", [2 * PAIRS, 2, DH])
        nullk_ss = sb("nullk_ss", [2 * PAIRS, 2])
        nullkT = sb("nullkT", [P, PAIRS, NULL])
        nullv = sb("nullv", [QB + NULL, INNER])
        iox = sb("iox", [P, EX, TOPK])
        ioy = sb("ioy", [P, NKEY, TOPK], fp16)
        spread = sb("spread", [NKEY + EX, EXPERTS], fp16)
        ident16 = sb("ident16", [P, P], fp16)
        hid = sb("hid", [P, TILES, DIM])

        oT = sb("oT", [P, PAIRS, TILES * P])
        scratch = oT[:].rearrange("p a n -> p (a n)")
        taken = [0]

        def early(*shape):
            n = 1
            for k in shape:
                n *= k
            taken[0] += n
            v = scratch[:, taken[0] - n:taken[0]]
            if len(shape) == 2:
                v = v.rearrange("p (a b) -> p a b", b=shape[1])
            elif len(shape) == 3:
                v = v.rearrange("p (a b c) -> p a b c", b=shape[1], c=shape[2])
            return v

        pat = early(GROUPS, PDIM)
        tokW_sb = early(PC, DIM)
        pT = early(2, PC, P)
        tk = early(GROUPS, DIM)
        anorm = early(2, TPG, DIM)
        xhat = early(2, TPG, DIM)
        p_st, p_mv, p_rs = early(GROUPS, 2, 6), early(GROUPS, 2), early(GROUPS)
        t_st, t_mv, t_rs = early(GROUPS, 6), early(GROUPS, 2), early(GROUPS)
        g_st, g_mv = early(GROUPS, TPG, 6), early(GROUPS, TPG, 2)
        g_rs, g_rs2, g_mr = early(GROUPS, TPG), early(GROUPS, TPG), early(GROUPS, TPG)

        Wq_sb = tmp("Wq_sb", [P, DC, INNER])
        Wkv_sb = tmp("Wkv_sb", [P, DC, 2 * INNER])
        dist = tmp("dist", [QB, SC])
        slope = tmp("slope", [QB, HEADS])
        aT_all = tmp("aT_all", [P, DC, TILES * P])
        xnT_all = tmp("xnT_all", [P, DC, TILES * P])
        aT = tmp("aT", [P, DC, TOK])
        xnT = tmp("xnT", [P, DC, TOK])
        aTv = tmp("aTv", [P, DC, TOK])
        sq = rows_sb[:].rearrange("p k n -> p (k n)")
        ss = tmp("ss", [P, 4 * TPG])
        rn = tmp("rn", [P, 4 * TPG])
        qk = tmp("qk", [P, 2, TPG * 2 * P])
        qT = tmp("qT", [P, 2, TOK])
        kT = tmp("kT", [P, 2, 2, KEYS])
        V = tmp("V", [KA, 2, 4, P])
        pbias = tmp("pbias", [QB, 2, SC])
        S = tmp("S", [QB, 2, SC])
        rowmin = tmp("rowmin", [QB, 8])
        rowsum = tmp("rowsum", [QB, 2, 8])
        rrec = tmp("rrec", [QB, 2, 8])
        probs = tmp("probs", [QB, 2, SC])
        pTs = tmp("pTs", [KA, 2, 3 * QB])
        O = tmp("O", [QB, 2, 4, P])

        phase.close()

        fst = tmp("fst", [P, 6])
        fmv = tmp("fmv", [P, 2])
        frs = tmp("frs", [P, 1])
        fn = tmp("fn", [P, DIM])
        fT = tmp("fT", [P, 2, DC, P])
        rqT = tmp("rqT", [P, RH, P])
        sim = tmp("sim", [P, 2, 2, RH, NKEY])
        act = tmp("act", [P, 2, FC, P])
        dot = tmp("dot", [P, 2, EXPERTS])
        top = tmp("top", [P, 2, RH, TOPK])
        tix = tmp("tix", [P, 2, RH, TOPK], u32)
        tixf = tmp("tixf", [P, RH, TOPK])
        tiy = tmp("tiy", [P, RH, TOPK], fp16)
        cand = tmp("cand", [P, RH, TOPK, TOPK])
        cand2 = tmp("cand2", [P, RH, TOPK, TOPK])
        best = tmp("best", [P, RH, TOPK])
        chosen = tmp("chosen", [P, RH, TOPK, TOPK])
        count = tmp("count", [P, RH, TOPK])
        epx = tmp("epx", [P, RH * (EX + NKEY + TOPK * TOPK)])
        zs = tmp("zs", [P, RH])
        rz = tmp("rz", [P, RH])
        exn = tmp("exn", [P, RH, EX])
        pc = tmp("pc", [P, RH, TOPK * TOPK])
        pcz = tmp("pcz", [P, RH, TOPK * TOPK])
        over = tmp("over", [P, RH, TOPK])
        chov = tmp("chov", [P, RH, TOPK, TOPK])
        wsil = tmp("wsil", [P, RH * TOPK * TOPK])
        wlast = tmp("wlast", [P, 1])
        ohx = tmp("ohx", [P, RH, EX, TOPK])
        dif = tmp("dif", [P, RH, NKEY, TOPK], fp16)
        nr = tmp("nr", [P, RH, NKEY + EX], fp16)
        nrT = tmp("nrT", [NKEY + EX, RH, P], fp16)
        oTs = tmp("oTs", [P, PAIRS, P])
        pxy = tmp("pxy", [P, RH, EX, NKEY])
        gsil = tmp("gsil", [P, 2, EX, NKEY])
        wh = tmp("wh", [P, 2, EXPERTS])
        wsum = tmp("wsum", [P, EXPERTS])
        wT = tmp("wT", [P, EC, P])

        phase.close()

        psum = ctx.enter_context(nc.psum_tensor("psum", [P, 8 * 512], fp32))
        bank = [psum[:, i * 512:(i + 1) * 512] for i in range(8)]

        ld_pat = [sem(f"ld_pat{g}") for g in range(GROUPS)]
        ld_rows = [sem(f"ld_rows{k}") for k in range(2)]
        ld_tok, ld_attn, ld_misc, ld_ffn, ld_txt, st_out = map(sem, (
            "ld_tok", "ld_attn", "ld_misc", "ld_ffn", "ld_txt", "st_out"))
        c_ident, c_pool, c_spread, c_bias, c_qks, c_null, c_nullT, c_nullk = map(sem, (
            "c_ident", "c_pool", "c_spread", "c_bias", "c_qks", "c_null", "c_nullT", "c_nullk"))
        p_stats, p_rstd, p_norm, t_tr, t_pT, t_mm, t_bias, t_stats, t_rstd, t_out = map(sem, (
            "p_stats", "p_rstd", "p_norm", "t_tr", "t_pT", "t_mm", "t_bias", "t_stats", "t_rstd", "t_out"))
        g_stats, g_rstd, g_norm, g_xhat, g_tr, g_T, g_slot, g_slotv = map(sem, (
            "g_stats", "g_rstd", "g_norm", "g_xhat", "g_tr", "g_T", "g_slot", "g_slotv"))
        a_qk, a_raw, a_v, a_sq, a_ss, a_rn, a_qkn, a_trq, a_trk, a_bias, a_qT, a_kT, a_nk, a_V, a_nv = map(sem, (
            "a_qk", "a_raw", "a_v", "a_sq", "a_ss", "a_rn", "a_qkn", "a_trq", "a_trk", "a_bias", "a_qT", "a_kT", "a_nk",
            "a_V", "a_nv"))
        a_sc, a_min, a_pr, a_trp, a_pT, a_pv, a_rec, a_on, a_tro, a_oT = map(sem, (
            "a_sc", "a_min", "a_pr", "a_trp", "a_pT", "a_pv", "a_rec", "a_on", "a_tro", "a_oT"))
        f_stats, f_rstd, f_norm, f_trf, f_fT, f_rq, f_rqT, f_simp, f_sim, f_up, f_act, f_dotp, f_dot = \
            map(sem, ("f_stats", "f_rstd", "f_norm", "f_trf", "f_fT", "f_rq", "f_rqT", "f_simp",
                      "f_sim", "f_up", "f_act", "f_dotp", "f_dot"))
        f_sel, f_arg, f_exn, f_pcz, f_exp, f_px, f_gate, f_sil, f_wh, f_sum, f_last, f_wsil, f_trw, f_wT, f_y, f_res, f_in, f_yo, f_hid, \
            f_nr, f_trn, f_nrT, f_dif = \
            map(sem, ("f_sel", "f_arg", "f_exn", "f_pcz", "f_exp", "f_px", "f_gate", "f_sil", "f_wh", "f_sum", "f_last",
                      "f_wsil", "f_trw", "f_wT", "f_y", "f_res", "f_in", "f_yo", "f_hid", "f_nr", "f_trn", "f_nrT",
                      "f_dif"))

        passed = {"dve": sem("passed_dve"), "pool": sem("passed_pool")}

        def wait_alone(engine, semaphore, value, name):
            engine.wait_ge(semaphore, value)
            engine.sem_inc(passed[name])

        def steps(engine, step):
            step(-1, 1, True, True, False, False)
            step(0, 0, True, True, True, False)
            with engine.Fori(0, TILES // 2 - 2) as tt:
                for k in range(1, 3):
                    step(tt * 2 + k, k % 2, True, True, True, True)
            step(TILES - 3, 1, True, True, True, True)
            step(TILES - 2, 0, False, True, True, True)
            step(TILES - 1, 1, False, False, True, True)
            step(TILES, 0, False, False, False, True)

        block = ctx.enter_context(nc.Block())

        @block.sync
        def _(sp):
            for g in range(GROUPS):
                sp.dma_start(pat[:, g, :], patches[g * P:(g + 1) * P, :]).then_inc(ld_pat[g], 16)
                if g == 0:
                    sp.dma_start(ln1g_sb[:], ln1_g).then_inc(ld_rows[0], 16)
                    sp.dma_start(ln1b_sb[:], ln1_b).then_inc(ld_rows[0], 16)
                    sp.dma_start(tokW_sb[:], tokW.rearrange("(c p) n -> p c n", p=P)).then_inc(ld_tok, 16)
            for k, row in enumerate((tok_b, ln2_g, ln2_b)):
                sp.dma_start(rows_sb[:, k, :], row).then_inc(ld_rows[1], 16)
            for g in range(GROUPS):
                sp.dma_start(hid[NPATCH:P, TPG * g, :], txt[2 * g, 0:NPATCH, :]).then_inc(ld_txt, 16)
                sp.dma_start(hid[0:NPATCH, TPG * g + 1, :], txt[2 * g, NPATCH:TXT, :]).then_inc(ld_txt, 16)
                sp.dma_start(hid[:, TPG * g + 2, :], txt[2 * g + 1, :, :]).then_inc(ld_txt, 16)
            for dst, src in ((qk_raw[:, 0:1], q_scale), (qk_raw[:, 1:2], k_scale),
                             (nullk[:].rearrange("r a d -> r (a d)"), null_k),
                             (nullv[QB:QB + NULL, :], null_v), (ng_sb[:], norm_g), (nb_sb[:], norm_b)):
                sp.dma_start(dst, src).then_inc(ld_misc, 16)
            for dst, src in ((Wq_sb, Wq), (Wkv_sb, Wkv), (Wout_sb, Wout)):
                sp.dma_start(dst[:], src.rearrange("(c p) n -> p c n", p=P)).then_inc(ld_attn, 16)
            for dst, src in ((Wr_sb, WrT), (Wup_sb, WupT), (down_sb, downT), (Wdn_sb, WdownT),
                             (up_sb, upE)):
                sp.dma_start(dst[:], src.rearrange("(c p) n -> p c n", p=P)).then_inc(ld_ffn, 16)
            sp.wait_ge(c_pool, 1)
            sp.dma_start(keyB[0:RN, :, 0:NKEY], keysT[0:RN]).then_inc(ld_ffn, 16)
            sp.dma_start(keyB[RN:P, :, NKEY:P], keysT[RN:P]).then_inc(ld_ffn, 16)

            def store(t):
                sp.wait_ge(f_res, t + 1)
                sp.dma_start(out[bass.ds(t, 1)].rearrange("a p d -> p (a d)"),
                             hid[:, bass.ds(t, 1), :].rearrange("p a d -> p (a d)")).then_inc(st_out, 16)

            def attended(t):
                sp.dma_start(oTs[:], oT[:, :, bass.ds(t * P, P)]).then_inc(f_in, 16)

            sp.wait_ge(a_oT, GROUPS * PAIRS + 1)
            attended(0)
            sp.wait_ge(f_yo, 1)
            attended(1)
            with sp.Fori(0, TILES - 2) as t:
                sp.wait_ge(f_yo, t + 2)
                attended(t + 2)
            with sp.Fori(0, TILES) as t:
                store(t)
            sp.wait_ge(st_out, 16 * TILES)

        @block.gpsimd
        def _(pool):
            nc.gpsimd.memset(keyB[:], 0.0).then_inc(c_pool, 1)
            nc.gpsimd.memset(ident[:], 0.0).then_inc(c_pool, 1)
            nc.gpsimd.memset(half[:], -0.5).then_inc(c_pool, 1)
            nc.gpsimd.memset(spread[:], 0.0).then_inc(c_pool, 1)
            nc.gpsimd.memset(ident16[:], 0.0).then_inc(c_pool, 1)
            pool.wait_ge(c_pool, 5)
            nc.gpsimd.affine_select(out=ident[:], in_=ident[:], compare_op=ALU.not_equal, fill=1.0, base=0,
                                    pattern=[[-1, P]], channel_multiplier=1).then_inc(c_ident, 1)
            nc.gpsimd.affine_select(out=ident16[:], in_=ident16[:], compare_op=ALU.not_equal, fill=1.0, base=0,
                                    pattern=[[-1, P]], channel_multiplier=1).then_inc(c_spread, 1)
            nc.gpsimd.affine_select(out=spread[0:NKEY], in_=spread[0:NKEY], compare_op=ALU.not_equal, fill=-1.0,
                                    base=0, pattern=[[0, EX], [-1, NKEY]], channel_multiplier=1).then_inc(c_spread, 1)
            pool.wait_ge(c_spread, 2)
            nc.gpsimd.affine_select(out=spread[NKEY:], in_=spread[NKEY:], compare_op=ALU.not_equal, fill=1.0,
                                    base=0, pattern=[[-1, EX], [0, NKEY]], channel_multiplier=1).then_inc(c_spread, 1)
            pool.wait_ge(c_spread, 3)

            pieces = ((0, QB, 0), (KA, QB, QB), (2 * KA, QB, 0))
            for at, n, base in pieces:
                nc.gpsimd.iota(dist[:, at:at + n], pattern=[[-1, n]], base=base, channel_multiplier=1,
                               allow_small_or_imprecise_dtypes=True).then_inc(c_pool, 1)
            for at, base in ((QB, NULL), (KA + QB, QB + NULL)):
                nc.gpsimd.iota(dist[:, at:at + NULL], pattern=[[-1, NULL]], base=base, channel_multiplier=1,
                               allow_small_or_imprecise_dtypes=True).then_inc(c_pool, 1)
            pool.wait_ge(c_pool, 10)
            for at in (0, 2 * KA):
                nc.gpsimd.affine_select(out=dist[:, at:at + QB], in_=dist[:, at:at + QB], compare_op=ALU.is_ge,
                                        fill=BIG, base=0, pattern=[[-1, QB]], channel_multiplier=1).then_inc(c_pool, 1)
            pool.wait_ge(c_pool, 12)
            start = 2.0 ** -0.5
            for h in range(HEADS):
                nc.gpsimd.memset(slope[:, h:h + 1], start * start ** h).then_inc(c_bias, 1)
            nc.gpsimd.iota(iox[:], pattern=[[1, EX], [0, TOPK]], base=0, channel_multiplier=0,
                           allow_small_or_imprecise_dtypes=True).then_inc(c_pool, 1)
            nc.gpsimd.iota(ioy[:], pattern=[[32, NKEY], [1, TOPK]], base=1, channel_multiplier=0,
                           allow_small_or_imprecise_dtypes=True).then_inc(c_pool, 1)

            def rstd(var, dst, before, done, scale=1.0, eps=EPS):
                pool.wait_ge(*before)
                nc.gpsimd.tensor_scalar(dst, var, scale, eps, ALU.mult, ALU.add).then_inc(done[0], 1)
                pool.wait_ge(done[0], done[1])
                nc.gpsimd.tensor_tensor(dst, dst, half[:, 0:dst.shape[-1]], ALU.pow).then_inc(done[0], 1)

            for g in range(GROUPS):
                rstd(p_mv[:, g, 1:2], p_rs[:, g:g + 1], (p_stats, 3 * g + 3), (p_rstd, 2 * g + 1))
            def token_rstd(g):
                rstd(t_mv[:, g, 1:2], t_rs[:, g:g + 1], (t_stats, 2 * g + 2), (t_rstd, 2 * g + 1))
            def block_rstd(g):
                var, mean = (g_mv[:, g, :, k:k + 1].rearrange("p t a -> p (t a)") for k in (1, 0))
                rstd(var, g_rs[:, g], (g_stats, 6 * g + 6), (g_rstd, 6 * g + 1))
                rstd(var, g_rs2[:, g], (g_stats, 6 * g + 6), (g_rstd, 6 * g + 3), 1.0 + EPS, EPS * EPS)
                pool.wait_ge(g_rstd, 6 * g + 4)
                nc.gpsimd.tensor_tensor(g_mr[:, g], g_rs2[:, g], mean, ALU.mult).then_inc(g_rstd, 1)
                pool.wait_ge(g_rstd, 6 * g + 5)
                nc.gpsimd.tensor_scalar(g_mr[:, g], g_mr[:, g], -1.0, None, ALU.mult).then_inc(g_rstd, 1)
            for g in range(GROUPS + 1):
                if g < GROUPS:
                    token_rstd(g)
                if g > 0:
                    block_rstd(g - 1)
            pool.wait_ge(c_null, 2)
            nc.gpsimd.tensor_scalar(nullk_ss[:], nullk_ss[:], 1e-24, None, ALU.max).then_inc(c_null, 1)
            pool.wait_ge(c_null, 3)
            nc.gpsimd.tensor_tensor(nullk_ss[:], nullk_ss[:], half[0:2 * PAIRS, 0:2], ALU.pow).then_inc(c_null, 1)

            def inv_norms(n):
                wait_alone(pool, a_ss, n + 1, "pool")
                nc.gpsimd.tensor_scalar(rn[:], ss[:], 1e-24, None, ALU.max).then_inc(a_rn, 1)
                pool.wait_ge(a_rn, 2 * n + 1)
                nc.gpsimd.tensor_tensor(rn[:], rn[:], half[:, 0:4 * TPG], ALU.pow).then_inc(a_rn, 1)
                wait_alone(pool, a_rn, 2 * n + 2, "pool")

            def null_keys(n, m, s):
                for b in range(2):
                    nc.gpsimd.tensor_copy(kT[:, s, b, QB:KA], nullkT[:, bass.ds(m, 1), :].rearrange("p a n -> p (a n)")).then_inc(a_nk, 1)
                wait_alone(pool, a_nk, 2 * n + 2, "pool")

            def null_values(n, m, s):
                for b in range(2):
                    nc.gpsimd.tensor_copy(V[QB:KA, s, 2 * b, :], nullv[QB:KA, bass.ds(m * P, P)]).then_inc(a_nv, 1)
                wait_alone(pool, a_nv, 2 * n + 2, "pool")

            def pair_bias(n, m, hh):
                nc.gpsimd.tensor_tensor(pbias[:, hh, :], dist[:], slope[:, bass.ds(m * 2 + hh, 1)].broadcast_to([QB, SC]),
                                        ALU.mult).then_inc(a_bias, 1)

            pool.wait_ge(c_bias, HEADS)
            pool.wait_ge(c_nullT, 2)
            pool.wait_ge(ld_misc, 96)
            inv_norms(0)
            inv_norms(1)
            for hh in range(2):
                pair_bias(0, 0, hh)
            null_keys(0, 0, 0)
            null_values(0, 0, 0)

            def pair(n, s, m1, norms):
                wait_alone(pool, a_min, 8 * n + 6, "pool")
                pair_bias(n + 1, m1, 0)
                null_keys(n + 1, m1, 1 - s)
                wait_alone(pool, a_min, 8 * n + 8, "pool")
                pair_bias(n + 1, m1, 1)
                if norms:
                    inv_norms(n + 2)
                wait_alone(pool, a_pv, 4 * n + 1, "pool")
                null_values(n + 1, m1, 1 - s)

            def group(n0, last):
                with pool.Fori(0, PAIRS // 2 - 1) as j:
                    for s in range(2):
                        pair(n0 + j * 2 + s, s, j * 2 + (s + 1), True)
                pair(n0 + (PAIRS - 2), 0, PAIRS - 1, not last)
                if not last:
                    pair(n0 + (PAIRS - 1), 1, 0, True)

            with pool.Fori(0, GROUPS - 1) as g:
                group(g * PAIRS, False)
            group((GROUPS - 1) * PAIRS, True)

            def ffn_norm(t):
                wait_alone(pool, f_stats, 2 * t + 2, "pool")
                nc.gpsimd.tensor_scalar(frs[:], fmv[:, 1:2], EPS, None, ALU.add).then_inc(f_rstd, 1)
                pool.wait_ge(f_rstd, 2 * t + 1)
                nc.gpsimd.tensor_tensor(frs[:], frs[:], half[:, 0:1], ALU.pow).then_inc(f_rstd, 1)

            def probabilities(t, h):
                if not isinstance(t, int) or t > 0:
                    pool.wait_ge(f_sil, 4 * t + h - 3)
                nc.gpsimd.tensor_tensor(
                    pxy[:, h], exn[:, h, :].unsqueeze(2).broadcast_to([P, EX, NKEY]),
                    epx[:, RH * EX + h * NKEY:RH * EX + (h + 1) * NKEY].unsqueeze(1).broadcast_to([P, EX, NKEY]),
                    ALU.mult).then_inc(f_px, 1)

            def add_head(t, h):
                pool.wait_ge(f_wh, 4 * t + h + 1)
                if h >= 2:
                    pool.wait_ge(f_sum, 3 * t + h - 1)
                elif not isinstance(t, int) or t > 0:
                    pool.wait_ge(f_trw, t)
                a = wh[:, 0, :] if h == 1 else wsum[:]
                nc.gpsimd.tensor_tensor(wsum[:], a, wh[:, h % 2, :], ALU.add).then_inc(f_sum, 1)

            def step(t, slot, a, b, c, d):
                if c:
                    add_head(t, 1)
                if a:
                    ffn_norm(t + 2)
                if c:
                    add_head(t, 2)
                    add_head(t, 3)
                if b:
                    pool.wait_ge(f_exn, t + 2)
                    for h in range(RH):
                        probabilities(t + 1, h)

            ffn_norm(0)
            steps(pool, step)

        @block.vector
        def _(dve):
            def patch_stats(g):
                dve.wait_ge(ld_pat[g], 16)
                for k in range(2):
                    nc.vector.bn_stats(p_st[:, g, k, :], pat[:, g, k * (PDIM // 2):(k + 1) * (PDIM // 2)]).then_inc(p_stats, 1)
                dve.wait_ge(p_stats, 3 * g + 2)
                nc.vector.bn_aggr(p_mv[:, g, :], p_st[:, g]).then_inc(p_stats, 1)

            def patch_norm(g):
                dve.wait_ge(p_rstd, 2 * g + 2)
                nc.vector.tensor_scalar(pat[:, g, :], pat[:, g, :], p_mv[:, g, 0:1], p_rs[:, g:g + 1], ALU.subtract,
                                        ALU.mult).then_inc(p_norm, 1)

            def token_stats(g):
                dve.wait_ge(t_mm, g + 1)
                nc.vector.tensor_tensor(tk[:, g, :], bank[6 + g % 2][:, 0:DIM], rows_sb[:, 0, :], ALU.add).then_inc(t_bias, 1)
                dve.wait_ge(t_bias, g + 1)
                nc.vector.bn_stats(t_st[:, g, :], tk[:, g, :]).then_inc(t_stats, 1)
                dve.wait_ge(t_stats, 2 * g + 1)
                nc.vector.bn_aggr(t_mv[:, g, :], t_st[:, g, :]).then_inc(t_stats, 1)

            def token_norm(g):
                x = tk[:, g, :]
                dve.wait_ge(t_rstd, 2 * g + 2)
                nc.vector.tensor_scalar(x, x, t_mv[:, g, 0:1], t_rs[:, g:g + 1], ALU.subtract, ALU.mult).then_inc(t_out, 1)
                dve.wait_ge(t_out, 4 * g + 1)
                nc.vector.tensor_tensor(x, x, rows_sb[:, 1, :], ALU.mult).then_inc(t_out, 1)
                dve.wait_ge(t_out, 4 * g + 2)
                for lo, tile in ((0, 0), (NPATCH, 1)):
                    nc.vector.tensor_tensor(hid[lo:lo + NPATCH, TPG * g + tile, :], tk[lo:lo + NPATCH, g, :],
                                            rows_sb[lo:lo + NPATCH, 2, :], ALU.add).then_inc(t_out, 1)
                dve.wait_ge(t_out, 4 * g + 4)
                for t in range(TPG):
                    nc.vector.bn_stats(g_st[:, g, t, :], hid[:, TPG * g + t, :]).then_inc(g_stats, 1)
                for t in range(TPG):
                    dve.wait_ge(g_stats, 6 * g + 1 + t)
                    nc.vector.bn_aggr(g_mv[:, g, t, :], g_st[:, g, t, :]).then_inc(g_stats, 1)

            def block_norm(g):
                dve.wait_ge(g_rstd, 6 * g + 2)
                if g >= 2:
                    dve.wait_ge(g_tr, 4 * (g - 2) + 2)
                for t in range(TPG):
                    nc.vector.tensor_scalar(anorm[:, g % 2, t, :],
                                            hid[:, TPG * g + t, :], g_mv[:, g, t, 0:1], g_rs[:, g, t:t + 1],
                                            ALU.subtract, ALU.mult).then_inc(g_norm, 1)

            for g in range(GROUPS + 1):
                if g < GROUPS:
                    patch_stats(g)
                if g > 0:
                    patch_norm(g - 1)
            dve.wait_ge(ld_rows[1], 16 * 3)
            dve.wait_ge(ld_txt, 16 * 3 * GROUPS)
            for g in range(GROUPS + 2):
                if g < GROUPS:
                    token_stats(g)
                if 0 < g <= GROUPS:
                    token_norm(g - 1)
                if g > 1:
                    block_norm(g - 2)
            dve.wait_ge(ld_misc, 96)
            nc.vector.tensor_tensor(qks[:], qk_raw[:, 0:1], qk_raw[:, 1:2], ALU.mult).then_inc(c_qks, 1)
            nc.vector.tensor_tensor(nullk_sq[:], nullk[:], nullk[:], ALU.mult).then_inc(c_null, 1)
            dve.wait_ge(c_qks, 1)
            nc.vector.tensor_scalar(qks[:], qks[:], -8.0, None, ALU.mult).then_inc(c_qks, 1)
            dve.wait_ge(c_null, 1)
            nc.vector.tensor_reduce(nullk_ss[:], nullk_sq[:], axis=AX.X, op=ALU.add).then_inc(c_null, 1)
            dve.wait_ge(c_null, 4)
            nc.vector.tensor_tensor(nullk[:], nullk[:], nullk_ss[:].unsqueeze(2).broadcast_to([2 * PAIRS, 2, DH]),
                                    ALU.mult).then_inc(c_nullk, 1)
            def qk_norms(n):
                dve.wait_ge(a_sq, n + 1)
                nc.vector.tensor_reduce(ss[:], sq.rearrange("p (a d) -> p a d", d=DH), axis=AX.X,
                                        op=ALU.add).then_inc(a_ss, 1)

            def qk_scale(n, s):
                dve.wait_ge(a_rn, 2 * n + 2)
                x = qk[:, s, :].rearrange("p (a d) -> p a d", d=DH)
                nc.vector.tensor_tensor(x, x, rn[:].unsqueeze(2).broadcast_to([P, 4 * TPG, DH]),
                                        ALU.mult).then_inc(a_qkn, 1)

            def row_min(n, u):
                b, hh = divmod(u, 2)
                if b == 0:
                    dve.wait_ge(a_bias, 2 * n + hh + 1)
                wait_alone(dve, a_sc, 4 * n + u + 1, "dve")
                for q, (lo, cnt) in enumerate(((0, KA), (KA, KEYS))):
                    col = (b * 2 + q) * 2 + hh
                    nc.vector.tensor_tensor_reduce(
                        out=S[:, u % 2, lo:lo + cnt], in0=bank[3 + u % 2][0:QB, lo:lo + cnt],
                        in1=pbias[:, hh, lo:lo + cnt],
                        scale=1.0, scalar=BIG, op0=ALU.add, op1=ALU.min,
                        accum_out=rowmin[:, col:col + 1]).then_inc(a_min, 1)

            def of_head(x, s, u):
                b, hh = divmod(u, 2)
                return x[:, s, 4 * b:4 * b + 4].rearrange("p (q h) -> p q h", h=2)[:, :, hh:hh + 1]

            def probs_copy(n, u, s):
                dve.wait_ge(a_trp, 4 * n + u + 1)
                nc.vector.reciprocal(of_head(rrec, s, u), of_head(rowsum, s, u)).then_inc(a_rec, 1)
                nc.vector.tensor_copy(pTs[:, u % 2, 0:2 * QB], bank[5 + u % 2][0:KA, 0:2 * QB]).then_inc(a_pT, 1)
                nc.vector.tensor_copy(pTs[0:QB, u % 2, 2 * QB:3 * QB],
                                      bank[5 + u % 2][0:QB, 2 * QB:3 * QB]).then_inc(a_pT, 1)

            def out_scale(n, u, s):
                b, hh = divmod(u, 2)
                dve.wait_ge(a_rec, 4 * n + u + 1)
                dve.wait_ge(a_pv, 4 * n + u + 1)
                nc.vector.tensor_tensor(O[:, s, 2 * b:2 * b + 2, hh * DH:(hh + 1) * DH],
                                        bank[5 + u % 2][0:QB, VAT:VAT + 2 * DH].rearrange("p (q d) -> p q d", d=DH),
                                        of_head(rrec, s, u).broadcast_to([QB, 2, DH]), ALU.mult).then_inc(a_on, 1)

            def operands(g):
                for dst, src in ((aT, aT_all), (xnT, xnT_all)):
                    nc.vector.tensor_copy(dst[:], src[:, :, bass.ds(g * TOK, TOK)]).then_inc(g_slot, 1)

            def operand_v(g):
                nc.vector.tensor_copy(aTv[:], aT_all[:, :, bass.ds(g * TOK, TOK)]).then_inc(g_slotv, 1)

            def pair(n, s, c1, c2, next_qk=None, next_v=None):
                probs_copy(n, 1, s)
                row_min(n, 3)
                out_scale(n, 0, s)
                if next_qk is not None:
                    wait_alone(dve, a_qk, 2 * n + 6, "dve")
                    operands(next_qk)
                if c2:
                    qk_norms(n + 2)
                probs_copy(n, 2, s)
                if c1:
                    row_min(n + 1, 0)
                out_scale(n, 1, s)
                if next_v is not None:
                    wait_alone(dve, a_v, n + 2, "dve")
                    operand_v(next_v)
                probs_copy(n, 3, s)
                if c1:
                    row_min(n + 1, 1)
                out_scale(n, 2, s)
                if c2:
                    qk_scale(n + 2, s)
                if c1:
                    probs_copy(n + 1, 0, 1 - s)
                    row_min(n + 1, 2)
                out_scale(n, 3, s)

            dve.wait_ge(g_T, 4 * GROUPS)
            operands(0)
            operand_v(0)
            for n in range(2):
                qk_norms(n)
                qk_scale(n, n)
            row_min(0, 0)
            row_min(0, 1)
            probs_copy(0, 0, 0)
            row_min(0, 2)

            def group(g, last):
                n0 = g * PAIRS
                with dve.Fori(0, PAIRS // 2 - 2) as j:
                    for s in range(2):
                        pair(n0 + j * 2 + s, s, True, True)
                pair(n0 + (PAIRS - 4), 0, True, True)
                pair(n0 + (PAIRS - 3), 1, True, True, next_qk=None if last else g + 1)
                pair(n0 + (PAIRS - 2), 0, True, not last, next_v=None if last else g + 1)
                pair(n0 + (PAIRS - 1), 1, not last, not last)

            with dve.Fori(0, GROUPS - 1) as g:
                group(g, False)
            group(GROUPS - 1, True)
            dve.wait_ge(a_oT, GROUPS * PAIRS + 1)

            def ffn_hid(t):
                dve.wait_ge(f_yo, t + 1)
                x = hid[:, bass.ds(t, 1), :].rearrange("p a d -> p (a d)")
                nc.vector.tensor_tensor(x, x, bank[6][:, 0:DIM], ALU.add).then_inc(f_hid, 1)
                wait_alone(dve, f_hid, t + 1, "dve")
                nc.vector.bn_stats(fst[:], x).then_inc(f_stats, 1)
                wait_alone(dve, f_stats, 2 * t + 1, "dve")
                nc.vector.bn_aggr(fmv[:], fst[:]).then_inc(f_stats, 1)

            def ffn_norm(t):
                dve.wait_ge(f_rstd, 2 * t + 2)
                nc.vector.tensor_scalar(fn[:], hid[:, bass.ds(t, 1), :].rearrange("p a d -> p (a d)"), fmv[:, 0:1],
                                        frs[:], ALU.subtract, ALU.mult).then_inc(f_norm, 1)

            def gates(t, slot, h):
                dve.wait_ge(f_px, 4 * t + h + 1)
                if h == 0:
                    dve.wait_ge(f_dot, 2 * t + 2)
                x = pxy[:, h].rearrange("p x y -> p (x y)")
                nc.vector.tensor_tensor(x, dot[:, slot, :], x, ALU.mult).then_inc(f_gate, 1)

            def weights(t, h):
                dve.wait_ge(f_sil, 4 * t + h + 1)
                dve.wait_ge(f_dif, 4 * t + h + 1)
                if h >= 2:
                    dve.wait_ge(f_sum, 3 * t + 1)
                nc.vector.scalar_tensor_tensor(
                    out=wh[:, h % 2, :], in0=psum[:, (h % 2) * EXPERTS:(h % 2 + 1) * EXPERTS], scalar=0.0,
                    in1=gsil[:, h % 2].rearrange("p x y -> p (x y)"), op0=ALU.is_ge, op1=ALU.mult).then_inc(f_wh, 1)

            def step(t, slot, a, b, c, d):
                done = [0]
                other = 1 - slot

                def sel(ins):
                    ins.then_inc(f_sel, 1)
                    done[0] += 1
                    return done[0]

                def after(k):
                    wait_alone(dve, f_sel, (t + 1) * SEL_LEN + k, "dve")

                nx, ny = RH * EX, RH * NKEY
                if b:
                    wait_alone(dve, f_sim, t + 2, "dve")
                    for p in range(2):
                        for h in range(RH):
                            k = sel(nc.vector.max(top[:, p, h, :], sim[:, other, p, h, :]))
                if c:
                    gates(t, slot, 0)
                    gates(t, slot, 1)
                    last_expert(t)
                    gates(t, slot, 2)
                if b:
                    after(k)
                    kc = sel(nc.vector.tensor_tensor(
                        cand[:], top[:, 0].unsqueeze(3).broadcast_to([P, RH, TOPK, TOPK]),
                        top[:, 1].unsqueeze(2).broadcast_to([P, RH, TOPK, TOPK]), ALU.add))
                    for p in range(2):
                        for h in range(RH):
                            ki = sel(nc.vector.max_index(tix[:, p, h, :], top[:, p, h, :], sim[:, other, p, h, :]))
                if c:
                    weights(t, 0)
                    gates(t, slot, 3)
                if b:
                    after(kc)
                    for h in range(RH):
                        kb = sel(nc.vector.max(best[:, h, :], cand[:, h].rearrange("p a b -> p (a b)")))
                    nc.vector.tensor_tensor(
                        epx[:, 0:nx].rearrange("p (h x) -> p h x", h=RH), sim[:, other, 0, :, 0:EX],
                        top[:, 0, :, 0:1].broadcast_to([P, RH, EX]), ALU.subtract).then_inc(f_arg, 1)
                    nc.vector.tensor_tensor(
                        epx[:, nx:nx + ny].rearrange("p (h y) -> p h y", h=RH), sim[:, other, 1],
                        top[:, 1, :, 0:1].broadcast_to([P, RH, NKEY]), ALU.subtract).then_inc(f_arg, 1)
                    after(kb)
                    for h in range(RH):
                        kr = sel(nc.vector.match_replace(out=cand2[:, h].rearrange("p a b -> p (a b)"),
                                                         in_to_replace=best[:, h, :],
                                                         in_values=cand[:, h].rearrange("p a b -> p (a b)"),
                                                         imm_value=-BIG))
                    nc.vector.tensor_tensor(
                        epx[:, nx + ny:].rearrange("p (h c) -> p h c", h=RH), cand[:].rearrange("p h a b -> p h (a b)"),
                        best[:, :, 0:1].broadcast_to([P, RH, TOPK * TOPK]), ALU.subtract).then_inc(f_arg, 1)
                if c:
                    weights(t, 1)
                if b:
                    kx = sel(nc.vector.tensor_copy(tixf[:], tix[:, 0]))
                    ky = sel(nc.vector.tensor_scalar(tiy[:], tix[:, 1], 32.0, None, ALU.mult))
                if a:
                    ffn_hid(t + 2)
                if b:
                    after(kr)
                    kh = sel(nc.vector.tensor_tensor(chosen[:], cand[:], cand2[:], ALU.not_equal))
                    after(ky)
                    ko = sel(nc.vector.tensor_tensor(
                        ohx[:], iox[:].unsqueeze(1).broadcast_to([P, RH, EX, TOPK]),
                        tixf[:].unsqueeze(2).broadcast_to([P, RH, EX, TOPK]), ALU.is_equal))
                    after(kh)
                    kn = sel(nc.vector.tensor_reduce(count[:], chosen[:], axis=AX.X, op=ALU.add))
                if a:
                    ffn_norm(t + 2)
                if c:
                    weights(t, 2)
                if b:
                    kd = sel(nc.vector.tensor_tensor(
                        dif[:], ioy[:].unsqueeze(1).broadcast_to([P, RH, NKEY, TOPK]),
                        tiy[:].unsqueeze(2).broadcast_to([P, RH, NKEY, TOPK]), ALU.subtract))
                    after(kn)
                    kq = sel(nc.vector.tensor_tensor(
                        ohx[:], ohx[:], count[:].unsqueeze(2).broadcast_to([P, RH, EX, TOPK]), ALU.mult))
                    kv = sel(nc.vector.tensor_scalar(over[:], tixf[:], float(EX), None, ALU.is_ge))
                if d:
                    finish(t - 1)
                if c:
                    weights(t, 3)
                if b:
                    after(kv)
                    sel(nc.vector.tensor_tensor(chov[:], chosen[:],
                                                over[:].unsqueeze(3).broadcast_to([P, RH, TOPK, TOPK]), ALU.mult))
                    dve.wait_ge(f_exp, t + 2)
                    kp = sel(nc.vector.tensor_tensor(pc[:], epx[:, nx + ny:].rearrange("p (h c) -> p h c", h=RH),
                                                     chosen[:].rearrange("p h a b -> p h (a b)"), ALU.mult))
                    nc.vector.tensor_reduce(nr[:, :, NKEY:], ohx[:], axis=AX.X, op=ALU.max).then_inc(f_nr, 1)
                    after(kp)
                    kz = sel(nc.vector.tensor_reduce(zs[:], pc[:], axis=AX.X, op=ALU.add))
                    after(kz)
                    kz = sel(nc.vector.reciprocal(rz[:], zs[:]))
                    after(kz)
                    nc.vector.tensor_tensor(exn[:], epx[:, 0:nx].rearrange("p (h x) -> p h x", h=RH),
                                            rz[:].unsqueeze(2).broadcast_to([P, RH, EX]), ALU.mult).then_inc(f_exn, 1)
                    nc.vector.tensor_tensor(pcz[:], pc[:], rz[:].unsqueeze(2).broadcast_to([P, RH, TOPK * TOPK]),
                                            ALU.mult).then_inc(f_pcz, 1)
                    nc.vector.tensor_reduce(nr[:, :, 0:NKEY], dif[:], axis=AX.X, op=ALU.min,
                                            apply_absolute_value=True).then_inc(f_nr, 1)
                    assert done[0] == SEL_LEN, done[0]
                if c:
                    add_last(t)

            def last_expert(t):
                wait_alone(dve, f_wsil, t + 1, "dve")
                if not isinstance(t, int) or t > 0:
                    wait_alone(dve, f_last, 2 * t, "dve")
                nc.vector.tensor_tensor_reduce(out=cand2[:].rearrange("p h a b -> p (h a b)"), in0=wsil[:], in1=chov[:].rearrange("p h a b -> p (h a b)"),
                                               scale=1.0, scalar=0.0, op0=ALU.mult, op1=ALU.add,
                                               accum_out=wlast[:]).then_inc(f_last, 1)

            def add_last(t):
                dve.wait_ge(f_sum, 3 * t + 3)
                nc.vector.tensor_tensor(wsum[:, EXPERTS - 1:EXPERTS], wsum[:, EXPERTS - 1:EXPERTS], wlast[:],
                                        ALU.add).then_inc(f_last, 1)

            def finish(t):
                dve.wait_ge(f_y, t + 1)
                x = hid[:, bass.ds(t, 1), :].rearrange("p a d -> p (a d)")
                nc.vector.tensor_tensor(x, x, bank[7][:, 0:DIM], ALU.add).then_inc(f_res, 1)

            ffn_hid(0)
            ffn_norm(0)
            steps(dve, step)

        @block.scalar
        def _(ac):
            def raw(n, k, s):
                cnt = (4 * P, 2 * P)[k]
                ac.wait_ge(a_qk, 2 * n + k + 1)
                nc.scalar.copy(qk[:, s, 4 * P * k:4 * P * k + cnt], bank[k][:, 0:cnt]).then_inc(a_raw, 1)

            def squares(n, s):
                ac.wait_ge(a_raw, 2 * n + 2)
                nc.scalar.activation(sq, qk[:, s, :], ACT.Square).then_inc(a_sq, 1)

            def exps(n, u, s):
                ac.wait_ge(a_min, 8 * n + 2 * u + 2)
                b, hh = divmod(u, 2)
                for q, (lo, cnt) in enumerate(((0, KA), (KA, KEYS))):
                    col = (b * 2 + q) * 2 + hh
                    nc.scalar.activation(probs[:, u % 2, lo:lo + cnt], S[:, u % 2, lo:lo + cnt], ACT.Exp,
                                         bias=rowmin[:, col:col + 1], scale=-1.0,
                                         accum_out=rowsum[:, s, col:col + 1]).then_inc(a_pr, 1)

            def qk_copies(n, s):
                ac.wait_ge(a_trq, n + 1)
                nc.scalar.activation(qT[:, s, :], bank[0][:, 0:TOK], ACT.Copy, scale=qks[:]).then_inc(a_qT, 1)
                ac.wait_ge(a_trk, n + 1)
                src = bank[1][:, 0:TOK].rearrange("p (b n) -> p b n", b=2)
                nc.scalar.copy(kT[:, s, :, 0:QB], src[:, :, 0:QB]).then_inc(a_kT, 1)
                nc.scalar.copy(kT[:, s, :, KA:KEYS], src[:, :, QB:N]).then_inc(a_kT, 1)

            def v_copy(n, s):
                ac.wait_ge(a_v, n + 1)
                nc.scalar.copy(V[0:QB, s].rearrange("p c d -> p (c d)"), bank[2][0:QB, :]).then_inc(a_V, 1)

            def pair(n, g, m, s, c1, c2, c3):
                exps(n, 3, s)
                if c1:
                    v_copy(n + 1, 1 - s)
                    exps(n + 1, 0, 1 - s)
                if c3:
                    raw(n + 3, 0, 1 - s)
                if c1:
                    exps(n + 1, 1, 1 - s)
                if c3:
                    raw(n + 3, 1, 1 - s)
                if c1:
                    exps(n + 1, 2, 1 - s)
                if c2:
                    qk_copies(n + 2, s)
                if c3:
                    squares(n + 3, 1 - s)
                ac.wait_ge(a_tro, n + 1)
                dst = oT[:, bass.ds(m, 1), bass.ds(g * TOK, TOK)].rearrange("p a n -> p (a n)")
                nc.scalar.copy(dst, bank[7][:, 0:TOK]).then_inc(a_oT, 1)

            ac.sem_inc(a_oT)

            def both_norms(g):
                ac.wait_ge(g_rstd, 6 * g + 6)
                if g >= 2:
                    ac.wait_ge(g_tr, 4 * (g - 2) + 4)
                for t in range(TPG):
                    nc.scalar.activation(xhat[:, g % 2, t, :], hid[:, TPG * g + t, :], ACT.Identity,
                                         bias=g_mr[:, g, t:t + 1], scale=g_rs2[:, g, t:t + 1]).then_inc(g_xhat, 1)

            def inputs_T(g):
                for c in range(DC):
                    ac.wait_ge(g_tr, g * 4 + c + 1)
                    nc.scalar.copy(aT_all[:, c, g * TOK:(g + 1) * TOK], bank[c][:, 0:TOK]).then_inc(g_T, 1)
                for c in range(DC):
                    ac.wait_ge(g_tr, g * 4 + 2 + c + 1)
                    nc.scalar.activation(xnT_all[:, c, g * TOK:(g + 1) * TOK], bank[2 + c][:, 0:TOK], ACT.Identity,
                                         bias=nb_sb[:, c:c + 1], scale=ng_sb[:, c:c + 1]).then_inc(g_T, 1)

            ac.wait_ge(ld_rows[0], 16 * 2)
            for g in range(GROUPS):
                ac.wait_ge(t_tr, g + 1)
                if g >= 2:
                    ac.wait_ge(t_mm, g - 1)
                for c in range(PC):
                    nc.scalar.activation(pT[:, g % 2, c, :], bank[2 * (g % 2) + c // 4][:, (c % 4) * P:(c % 4 + 1) * P],
                                         ACT.Identity, bias=ln1b_sb[:, c:c + 1], scale=ln1g_sb[:, c:c + 1]).then_inc(t_pT, 1)
            ac.wait_ge(ld_misc, 96)
            for g in range(GROUPS + 1):
                if g < GROUPS:
                    both_norms(g)
                if g > 0:
                    inputs_T(g - 1)
            ac.wait_ge(c_qks, 2)
            ac.wait_ge(c_nullT, 1)
            nc.scalar.copy(nullkT[:].rearrange("p m n -> p (m n)"), bank[7][:, 0:2 * PAIRS]).then_inc(c_nullT, 1)

            for k in range(2):
                raw(0, k, 0)
            squares(0, 0)
            v_copy(0, 0)
            for k in range(2):
                raw(1, k, 1)
            ac.wait_ge(a_ss, 1)
            squares(1, 1)
            qk_copies(0, 0)
            exps(0, 0, 0)
            exps(0, 1, 0)
            for k in range(2):
                raw(2, k, 0)
            exps(0, 2, 0)
            qk_copies(1, 1)
            ac.wait_ge(a_ss, 2)
            squares(2, 0)

            def group(g, last):
                n0 = g * PAIRS
                with ac.Fori(0, PAIRS // 2 - 2) as j:
                    for s in range(2):
                        pair(n0 + j * 2 + s, g, j * 2 + s, s, True, True, True)
                for m in range(PAIRS - 4, PAIRS):
                    c1, c2, c3 = (not last or m < PAIRS - k for k in range(1, 4))
                    pair(n0 + m, g, m, m % 2, c1, c2, c3)

            with ac.Fori(0, GROUPS - 1) as g:
                group(g, False)
            group(GROUPS - 1, True)

            def fT_copy(t, slot):
                ac.wait_ge(f_trf, t + 1)
                nc.scalar.copy(fT[:, slot].rearrange("p c n -> p (c n)"), bank[6][:, DIM:2 * DIM]).then_inc(f_fT, 1)

            def rq_copy(t):
                ac.wait_ge(f_rq, t + 1)
                nc.scalar.copy(rqT[:].rearrange("p c n -> p (c n)"), bank[4][:]).then_inc(f_rqT, 1)

            def sim_copy(t, slot):
                ac.wait_ge(f_simp, t + 1)
                nc.scalar.copy(sim[:, slot].rearrange("p a h k -> p (a h k)"), bank[5][:]).then_inc(f_sim, 1)

            def dot_copy(t, slot, k):
                ac.wait_ge(f_dotp, 2 * t + k + 1)
                nc.scalar.copy(dot[:, slot, k * 512:(k + 1) * 512], bank[6 + k][:]).then_inc(f_dot, 1)

            def dense_silu(t, slot):
                for k in range(2):
                    ac.wait_ge(f_up, 2 * t + k + 1)
                    nc.scalar.activation(act[:, slot, 4 * k:4 * k + 4, :].rearrange("p c n -> p (c n)"), bank[4 + k][:],
                                         ACT.Silu).then_inc(f_act, 1)

            def silu(t, h):
                ac.wait_ge(f_gate, 4 * t + h + 1)
                if h >= 2:
                    ac.wait_ge(f_wh, 4 * t + h - 1)
                nc.scalar.activation(gsil[:, h % 2].rearrange("p x y -> p (x y)"),
                                     pxy[:, h].rearrange("p x y -> p (x y)"), ACT.Silu).then_inc(f_sil, 1)

            def w_copies(t):
                ac.wait_ge(f_trw, t + 1)
                for k in range(2):
                    nc.scalar.copy(wT[:, 4 * k:4 * k + 4, :].rearrange("p c n -> p (c n)"), bank[4 + k][:]).then_inc(f_wT, 1)

            def step(t, slot, a, b, c, d):
                other = 1 - slot
                if c:
                    silu(t, 0)
                    silu(t, 1)
                if c:
                    silu(t, 2)
                if d:
                    w_copies(t - 1)
                if c:
                    silu(t, 3)
                if b:
                    ac.wait_ge(f_arg, 3 * t + 6)
                    nc.scalar.activation(epx[:], epx[:], ACT.Exp).then_inc(f_exp, 1)
                if a:
                    fT_copy(t + 2, slot)
                    rq_copy(t + 2)
                if b:
                    dot_copy(t + 1, other, 0)
                if a:
                    sim_copy(t + 2, slot)
                if b:
                    dot_copy(t + 1, other, 1)
                    ac.wait_ge(f_trn, t + 2)
                    nc.scalar.copy(nrT[:].rearrange("r h n -> r (h n)"),
                                   bank[7][0:NKEY + EX, 0:DIM].bitcast(fp16)).then_inc(f_nrT, 1)
                    dense_silu(t + 1, other)
                    ac.wait_ge(f_pcz, t + 2)
                    ac.wait_ge(f_dot, 2 * t + 4)
                    nc.scalar.activation(wsil[:], pcz[:].rearrange("p h c -> p (h c)"), ACT.Silu,
                                         scale=dot[:, other, EXPERTS - 1:EXPERTS]).then_inc(f_wsil, 1)

            fT_copy(0, 0)
            rq_copy(0)
            sim_copy(0, 0)
            steps(ac, step)

        @block.tensor
        def _(pe):
            mm = nc.tensor.matmul
            pe.wait_ge(c_ident, 1)
            pe.wait_ge(ld_tok, 16)

            def patches_T(g):
                pe.wait_ge(p_norm, g + 1)
                if g >= 2:
                    pe.wait_ge(t_pT, PC * (g - 1))
                for c in range(PC):
                    last = nc.tensor.transpose(bank[2 * (g % 2) + c // 4][:, (c % 4) * P:(c % 4 + 1) * P],
                                               pat[:, g, c * P:(c + 1) * P], ident[:])
                last.then_inc(t_tr, 1)

            def tokens(g):
                pe.wait_ge(t_pT, PC * g + PC)
                if g >= 2:
                    pe.wait_ge(t_bias, g - 1)
                for c in range(PC):
                    last = mm(bank[6 + g % 2][:, 0:DIM], pT[:, g % 2, c, :], tokW_sb[:, c, :], start=(c == 0),
                              stop=(c == PC - 1))
                last.then_inc(t_mm, 1)

            for g in range(GROUPS + 1):
                if g < GROUPS:
                    patches_T(g)
                if g > 0:
                    tokens(g - 1)
            for g in range(GROUPS):
                for k, (src, done) in enumerate(((anorm, g_norm), (xhat, g_xhat))):
                    pe.wait_ge(done, TPG * (g + 1))
                    if g > 0:
                        pe.wait_ge(g_T, 4 * (g - 1) + 2 * k + 2)
                    for c in range(DC):
                        for t in range(TPG):
                            last = nc.tensor.transpose(bank[2 * k + c][:, t * P:(t + 1) * P],
                                                       src[:, g % 2, t, c * P:(c + 1) * P], ident[:])
                        last.then_inc(g_tr, 1)
            pe.wait_ge(c_nullk, 1)
            nc.tensor.transpose(bank[7][:, 0:2 * PAIRS], nullk[:].rearrange("r a d -> r (a d)"),
                                ident[0:2 * PAIRS, 0:2 * PAIRS]).then_inc(c_nullT, 1)
            pe.wait_ge(ld_attn, 48)

            def project_qk(n, m, tiles):
                for t in tiles:
                    for j, (lhs, w) in enumerate(((xnT, Wq_sb), (aT, Wkv_sb))):
                        for c in range(DC):
                            last = mm(bank[t // 2][:, ((t % 2) * 2 + j) * P:((t % 2) * 2 + j + 1) * P],
                                      lhs[:, c, t * P:(t + 1) * P], w[:, c, bass.ds(m * P, P)],
                                      start=(c == 0), stop=(c == DC - 1))
                    if t:
                        last.then_inc(a_qk, 1)

            def project_v(n, m, blocks):
                for b in blocks:
                    for c in range(DC):
                        last = mm(bank[2][0:QB, b * P:(b + 1) * P], aTv[:, c, b * QB:(b + 1) * QB],
                                  Wkv_sb[:, c, bass.ds(m * P + INNER, P)], start=(c == 0), stop=(c == DC - 1))
                if b == 3:
                    last.then_inc(a_v, 1)

            def scores(n, u, s):
                b, hh = divmod(u, 2)
                lo = hh * DH
                for q, (at, cnt) in enumerate(((0, KA), (KA, KEYS))):
                    last = mm(bank[3 + u % 2][0:QB, at:at + cnt],
                              qT[lo:lo + DH, s, b * N + q * QB:b * N + (q + 1) * QB], kT[lo:lo + DH, s, b, 0:cnt],
                              start=True, stop=True)
                last.then_inc(a_sc, 1)

            def probs_T(n, u):
                pe.wait_ge(a_pr, 8 * n + 2 * u + 2)
                pe.wait_ge(a_on, 4 * n + u + 1)
                for k, (at, cnt) in enumerate(((0, KA), (KA, KA), (2 * KA, QB))):
                    last = nc.tensor.transpose(bank[5 + u % 2][0:cnt, k * QB:(k + 1) * QB],
                                               probs[:, u % 2, at:at + cnt], ident[0:QB, 0:QB])
                last.then_inc(a_trp, 1)

            def values(n, u, s):
                b, hh = divmod(u, 2)
                if u == 0:
                    pe.wait_ge(a_V, n + 1)
                    pe.wait_ge(a_nv, 2 * n + 2)
                pe.wait_ge(a_pT, 8 * n + 2 * u + 2)
                vv = [V[0:KA, s, 2 * b, hh * DH:(hh + 1) * DH], V[0:QB, s, 2 * b + 1, hh * DH:(hh + 1) * DH]]
                pp = pTs[:, u % 2]
                o = [bank[5 + u % 2][0:QB, VAT + q * DH:VAT + (q + 1) * DH] for q in range(2)]
                mm(o[0], pp[:, 0:QB], vv[0], start=True, stop=True)
                mm(o[1], pp[:, QB:2 * QB], vv[0], start=True, stop=False)
                mm(o[1], pp[0:QB, 2 * QB:3 * QB], vv[1], start=False, stop=True).then_inc(a_pv, 1)

            def qk_T(n, s):
                pe.wait_ge(a_raw, min_raw(n))
                pe.wait_ge(a_qkn, n + 1)
                for j, done in enumerate((a_trq, a_trk)):
                    for t in range(TPG):
                        last = nc.tensor.transpose(bank[j][:, t * P:(t + 1) * P],
                                                   qk[:, s, (2 * t + j) * P:(2 * t + j + 1) * P], ident[:])
                    last.then_inc(done, 1)

            def min_raw(n):
                return 2 * n + 4 if not isinstance(n, int) or n < GROUPS * PAIRS - 1 else 2 * n + 2

            def out_T(n, s):
                pe.wait_ge(a_oT, n + 1)
                pe.wait_ge(a_on, 4 * n + 6)
                for c in range(4):
                    last = nc.tensor.transpose(bank[7][:, c * QB:(c + 1) * QB], O[:, s, c, :], ident[0:QB, 0:QB])
                last.then_inc(a_tro, 1)

            def first_scores(n, u, s):
                if u == 0:
                    pe.wait_ge(a_qT, n + 1)
                    pe.wait_ge(a_kT, 2 * n + 2)
                    pe.wait_ge(a_nk, 2 * n + 2)
                scores(n, u, s)

            def pair(n, s, m1, m2, m3, slot=None, slotv=None):
                probs_T(n, 1)
                scores(n, 3, s)
                values(n, 0, s)
                if m1 is not None:
                    project_v(n + 1, m1, (2, 3))
                probs_T(n, 2)
                if m1 is not None:
                    first_scores(n + 1, 0, 1 - s)
                values(n, 1, s)
                if m3 is not None:
                    if slot is not None:
                        pe.wait_ge(g_slot, slot)
                    project_qk(n + 3, m3, (0, 1))
                probs_T(n, 3)
                if m1 is not None:
                    first_scores(n + 1, 1, 1 - s)
                values(n, 2, s)
                if m3 is not None:
                    project_qk(n + 3, m3, (2,))
                if m1 is not None:
                    probs_T(n + 1, 0)
                    scores(n + 1, 2, 1 - s)
                values(n, 3, s)
                if m2 is not None:
                    qk_T(n + 2, s)
                    pe.wait_ge(a_V, n + 2)
                    if slotv is not None:
                        pe.wait_ge(g_slotv, slotv)
                    project_v(n + 2, m2, (0, 1))
                out_T(n, s)

            for _ in range(2):
                pe.sem_inc(a_on)
            pe.wait_ge(g_slot, 2)
            project_qk(0, 0, range(TPG))
            pe.wait_ge(g_slotv, 1)
            project_v(0, 0, range(4))
            pe.wait_ge(a_raw, 2)
            project_qk(1, 1, range(TPG))
            qk_T(0, 0)
            first_scores(0, 0, 0)
            first_scores(0, 1, 0)
            project_qk(2, 2, range(TPG))
            probs_T(0, 0)
            scores(0, 2, 0)
            qk_T(1, 1)
            pe.wait_ge(a_V, 1)
            project_v(1, 1, (0, 1))

            def group(g, last):
                n0 = g * PAIRS
                with pe.Fori(0, PAIRS // 2 - 2) as j:
                    for s in range(2):
                        pair(n0 + j * 2 + s, s, j * 2 + (s + 1), j * 2 + (s + 2), j * 2 + (s + 3))
                for m in range(PAIRS - 4, PAIRS):
                    nxt = [None if last and m + k >= PAIRS else (m + k) % PAIRS for k in range(1, 4)]
                    pair(n0 + m, m % 2, *nxt, slot=2 * g + 4 if m == PAIRS - 3 and not last else None,
                         slotv=g + 2 if m == PAIRS - 2 and not last else None)

            with pe.Fori(0, GROUPS - 1) as g:
                group(g, False)
            group(GROUPS - 1, True)

            pe.wait_ge(ld_ffn, 16 * 7)
            pe.wait_ge(c_spread, 3)

            def out_projection(t):
                pe.wait_ge(f_in, 16 * t + 16)
                for c in range(PAIRS):
                    last = mm(bank[6][:, 0:DIM], oTs[:, c, :], Wout_sb[:, c, :], start=(c == 0), stop=(c == PAIRS - 1))
                last.then_inc(f_yo, 1)

            def f_T(t):
                pe.wait_ge(f_norm, t + 1)
                for c in range(DC):
                    last = nc.tensor.transpose(bank[6][:, DIM + c * P:DIM + (c + 1) * P], fn[:, c * P:(c + 1) * P], ident[:])
                last.then_inc(f_trf, 1)

            def retrieval_q(t, slot):
                pe.wait_ge(f_fT, t + 1)
                for j in range(RH):
                    for c in range(DC):
                        last = mm(bank[4][:, j * P:(j + 1) * P], Wr_sb[:, c, j * P:(j + 1) * P], fT[:, slot, c, :],
                                  start=(c == 0), stop=(c == DC - 1))
                last.then_inc(f_rq, 1)

            def expert_dots(t, slot, k):
                for c in range(DC):
                    last = mm(bank[6 + k][:], fT[:, slot, c, :], down_sb[:, c, k * 512:(k + 1) * 512],
                              start=(c == 0), stop=(c == DC - 1))
                last.then_inc(f_dotp, 1)

            def key_scores(t):
                pe.wait_ge(f_rqT, t + 1)
                for j in range(RH):
                    last = mm(bank[5][:, j * P:(j + 1) * P], rqT[:, j, :], keyB[:, j, :], start=True, stop=True)
                last.then_inc(f_simp, 1)

            def dense_up(t, slot, k):
                for j in range(4):
                    f = 4 * k + j
                    for c in range(DC):
                        last = mm(bank[4 + k][:, j * P:(j + 1) * P], Wup_sb[:, c, f * P:(f + 1) * P], fT[:, slot, c, :],
                                  start=(c == 0), stop=(c == DC - 1))
                last.then_inc(f_up, 1)

            def count_less_rank(t, h):
                for k in range(2):
                    last = mm(bank[2 * (h % 2) + k][:], nrT[:, h, :], spread[:, k * 512:(k + 1) * 512], start=True,
                              stop=True)
                last.then_inc(f_dif, 1)

            def step(t, slot, a, b, c, d):
                other = 1 - slot
                if c:
                    pe.wait_ge(f_nrT, t + 1)
                    if d:
                        pe.wait_ge(f_wh, 4 * t)
                    count_less_rank(t, 0)
                    count_less_rank(t, 1)
                if c:
                    pe.wait_ge(f_act, 2 * t + 2)
                if d:
                    pe.wait_ge(f_last, 2 * t)
                    for e in range(EC):
                        last = nc.tensor.transpose(bank[4 + e // 4][:, (e % 4) * P:(e % 4 + 1) * P],
                                                   wsum[:, e * P:(e + 1) * P], ident[:])
                    last.then_inc(f_trw, 1)
                if a:
                    if c:
                        pe.wait_ge(f_dot, 2 * t + 2)
                    out_projection(t + 2)
                if d:
                    if not c:
                        pe.wait_ge(f_res, t - 1)
                    for k in range(FC):
                        mm(bank[7][:, 0:DIM], act[:, other, k, :], Wdn_sb[:, k, :], start=(k == 0), stop=False)
                if c:
                    for h in range(2, RH):
                        pe.wait_ge(f_wh, 4 * t + h - 1)
                        count_less_rank(t, h)
                if d:
                    pe.wait_ge(f_wT, 2 * t)
                    for e in range(EC):
                        last = mm(bank[7][:, 0:DIM], wT[:, e, :], up_sb[:, e, :], start=False, stop=(e == EC - 1))
                    last.then_inc(f_y, 1)
                if a:
                    f_T(t + 2)
                    retrieval_q(t + 2, slot)
                if b:
                    expert_dots(t + 1, other, 0)
                if a:
                    key_scores(t + 2)
                if b:
                    if d:
                        pe.wait_ge(f_res, t)
                    expert_dots(t + 1, other, 1)
                    dense_up(t + 1, other, 0)
                    pe.wait_ge(f_nr, 2 * t + 4)
                    pe.wait_ge(f_dot, 2 * t + 4)
                    for h in range(RH):
                        last = nc.tensor.transpose(bank[7][0:NKEY + EX, 0:DIM].bitcast(fp16)[:, h * P:(h + 1) * P],
                                                   nr[:, h, :], ident16[:])
                    last.then_inc(f_trn, 1)
                    if a:
                        pe.wait_ge(f_sim, t + 3)
                    dense_up(t + 1, other, 1)

            out_projection(0)
            f_T(0)
            retrieval_q(0, 0)
            key_scores(0)
            steps(pe, step)


_INS = ("patches", "txt", "ln1_g", "ln1_b", "tokW", "tok_b", "ln2_g", "ln2_b", "norm_g", "norm_b", "Wq", "Wkv",
        "q_scale", "k_scale", "null_k", "null_v", "Wout", "WupT", "WdownT", "WrT", "keysT", "downT", "upE")


def kernel(**inputs):
    import numpy as np
    import concourse.bacc as bacc
    from concourse.bass_utils import run_bass_kernel_spmd

    a = {k: np.asarray(v) for k, v in inputs.items()}

    def rows(v):
        return np.broadcast_to(v[None, :], (P, v.shape[0]))

    def by_feature(v):
        return v.reshape(-1, P).T

    null = a["L0_attn_null_kv"].reshape(PAIRS, 2, NULL, 2, DH)
    laid = {
        "patches": a["x"].reshape(B, CH, GRID, PATCH, GRID, PATCH).transpose(0, 2, 4, 3, 5, 1).reshape(B * NPATCH, PDIM),
        "txt": a["txt"],
        "ln1_g": by_feature(a["L0_tok_ln1_g"]), "ln1_b": by_feature(a["L0_tok_ln1_b"]), "tokW": a["L0_tok_W"],
        "tok_b": rows(a["L0_tok_b"]), "ln2_g": rows(a["L0_tok_ln2_g"]), "ln2_b": rows(a["L0_tok_ln2_b"]),
        "norm_g": by_feature(a["L0_attn_norm_g"]), "norm_b": by_feature(a["L0_attn_norm_b"]),
        "Wq": a["L0_attn_Wq"], "Wkv": a["L0_attn_Wkv"],
        "q_scale": np.tile(a["L0_attn_q_scale"], 2)[:, None], "k_scale": np.tile(a["L0_attn_k_scale"], 2)[:, None],
        "null_k": null[:, :, :, 0].transpose(0, 2, 1, 3).reshape(PAIRS * NULL, 2 * DH),
        "null_v": null[:, :, :, 1].transpose(2, 0, 1, 3).reshape(NULL, INNER),
        "Wout": a["L0_attn_Wout"], "WupT": a["L0_ffn_W_up"].T, "WdownT": a["L0_ffn_W_down"].T,
        "WrT": a["L0_ffn_W_q"].T,
        "keysT": a["L0_ffn_keys"].reshape(2, 2, NKEY, 2, RN).transpose(1, 4, 3, 0, 2).reshape(2 * RN, RH, NKEY),
        "downT": a["L0_ffn_down_embed"].T, "upE": a["L0_ffn_up_embed"],
    }
    nc = bacc.Bacc("TRN2", target_bir_lowering=False, num_devices=1)
    arrays, args = {}, []
    for name in _INS:
        arrays[name] = np.ascontiguousarray(laid[name])
        args.append(nc.dram_tensor(name, arrays[name].shape, mybir.dt.from_np(arrays[name].dtype),
                                   kind="ExternalInput").ap())
    out = nc.dram_tensor("out", (B, N, DIM), mybir.dt.float32, kind="ExternalOutput").ap()
    build_program(nc, *args, out.rearrange("b n d -> (b n) d").rearrange("(t p) d -> t p d", p=P))
    r = run_bass_kernel_spmd(nc, [arrays], core_ids=[0])
    return r.results[0]["out"]
```

```python
from contextlib import ExitStack

import concourse.bass as bass
from concourse import mybir

B, TXT, DIM = 8, 128, 256
GRID, PATCH, CH = 8, 16, 3
NPATCH = GRID * GRID
PDIM = CH * PATCH * PATCH
N = NPATCH + TXT
P = 128
TILES = B * N // P
GROUPS = 4
TPG = TILES // GROUPS
TOK = TPG * P
HEADS, DH, NULL = 16, 64, 2
PAIRS = HEADS // 2
INNER = HEADS * DH
QB = N // 2
KA = QB + NULL
KEYS = N + NULL
SC = KA + KEYS
DC = DIM // P
PC = PDIM // P
FF = 1024
FC = FF // P
RH, RN, NKEY, TOPK = 4, 64, 64, 8
EXPERTS = 1024
EX = EXPERTS // NKEY
EC = EXPERTS // P
SEL_LEN = 31
EPS = 1e-5
BIG = 3.0e38


def build_program(nc, patches, txt, ln1_g, ln1_b, tokW, tok_b, ln2_g, ln2_b, norm_g, norm_b, Wq, Wkv,
                  q_scale, k_scale, null_k, null_v, Wout, WupT, WdownT, Wr, keysT, downT, upE, out):
    fp32, fp16, u32 = mybir.dt.float32, mybir.dt.float16, mybir.dt.uint32
    ALU = mybir.AluOpType
    ACT = mybir.ActivationFunctionType
    AX = mybir.AxisListType

    ctx = ExitStack()
    with ctx:
        phase = ExitStack()

        def sb(name, shape, dt=fp32):
            return ctx.enter_context(nc.sbuf_tensor(name, shape, dt))

        def tmp(name, shape, dt=fp32):
            return phase.enter_context(nc.sbuf_tensor(name, shape, dt))

        def sem(name):
            return ctx.enter_context(nc.semaphore(name))

        ln1g_sb = sb("ln1g_sb", [P, PC])
        ln1b_sb = sb("ln1b_sb", [P, PC])
        rows_sb = sb("rows_sb", [P, 3, DIM])
        ng_sb = sb("ng_sb", [P, DC])
        nb_sb = sb("nb_sb", [P, DC])
        Wup_sb = sb("Wup_sb", [P, DC, FF])
        Wdn_sb = sb("Wdn_sb", [P, FC, DIM])
        simW = sb("simW", [P, DC, RH * P])
        Wout_sb = sb("Wout_sb", [P, PAIRS, DIM])
        down_sb = sb("down_sb", [P, DC, EXPERTS])
        up_sb = sb("up_sb", [P, EC, DIM])
        ident = sb("ident", [P, P])
        qk_raw = sb("qk_raw", [P, 2])
        qks = sb("qks", [P, 1])
        half = sb("half", [P, 16])
        nullk = sb("nullk", [2 * PAIRS, 2, DH])
        nullk_sq = sb("nullk_sq", [2 * PAIRS, 2, DH])
        nullk_ss = sb("nullk_ss", [2 * PAIRS, 2])
        nullkT = sb("nullkT", [P, PAIRS, NULL])
        nullv = sb("nullv", [QB + NULL, INNER])
        iox = sb("iox", [P, EX, TOPK])
        ioy = sb("ioy", [P, NKEY, TOPK], fp16)
        spread = sb("spread", [NKEY + EX, EXPERTS], fp16)
        ident16 = sb("ident16", [P, P], fp16)
        hid = sb("hid", [P, TILES, DIM])

        fst = sb("fst", [P, 6])
        fmv = sb("fmv", [P, 2])
        frs = sb("frs", [P, 1])
        fn = sb("fn", [P, DIM])
        fT = sb("fT", [P, 2, DC, P])
        sim = sb("sim", [P, 2, 2, RH, NKEY])

        oT = sb("oT", [P, PAIRS, TILES * P])
        scratch = oT[:].rearrange("p a n -> p (a n)")
        taken = [0]

        def early(*shape):
            n = 1
            for k in shape:
                n *= k
            taken[0] += n
            v = scratch[:, taken[0] - n:taken[0]]
            if len(shape) == 2:
                v = v.rearrange("p (a b) -> p a b", b=shape[1])
            elif len(shape) == 3:
                v = v.rearrange("p (a b c) -> p a b c", b=shape[1], c=shape[2])
            return v

        pat = early(GROUPS, PDIM)
        tokW_sb = early(PC, DIM)
        pT = early(2, PC, P)
        tk = early(GROUPS, DIM)
        anorm = early(2, TPG, DIM)
        xhat = early(2, TPG, DIM)
        Wr_sb = early(RH, DIM)
        keyB = early(RH, P)
        p_st, p_mv, p_rs = early(GROUPS, 2, 6), early(GROUPS, 2), early(GROUPS)
        t_st, t_mv, t_rs = early(GROUPS, 6), early(GROUPS, 2), early(GROUPS)
        g_st, g_mv = early(GROUPS, TPG, 6), early(GROUPS, TPG, 2)
        g_rs, g_rs2, g_mr = early(GROUPS, TPG), early(GROUPS, TPG), early(GROUPS, TPG)

        Wq_sb = tmp("Wq_sb", [P, DC, INNER])
        Wkv_sb = tmp("Wkv_sb", [P, DC, 2 * INNER])
        dist = tmp("dist", [QB, SC])
        slope = tmp("slope", [QB, HEADS])
        aT_all = tmp("aT_all", [P, DC, TILES * P])
        xnT_all = tmp("xnT_all", [P, DC, TILES * P])
        aT = tmp("aT", [P, DC, TOK])
        xnT = tmp("xnT", [P, DC, TOK])
        aTv = tmp("aTv", [P, DC, TOK])
        sq = rows_sb[:].rearrange("p k n -> p (k n)")
        ss = tmp("ss", [P, 4 * TPG])
        rn = tmp("rn", [P, 4 * TPG])
        qk = tmp("qk", [P, 2, TPG * 2 * P])
        qT = tmp("qT", [P, 2, TOK])
        kT = tmp("kT", [P, 2, 2, KEYS])
        V = tmp("V", [KA, 2, 4, P])
        pbias = tmp("pbias", [QB, 2, SC])
        S = tmp("S", [QB, 2, SC])
        rowmin = tmp("rowmin", [QB, 8])
        rowsum = tmp("rowsum", [QB, 2, 8])
        rrec = tmp("rrec", [QB, 2, 8])
        probs = tmp("probs", [QB, 2, SC])
        pTs = tmp("pTs", [KA, 2, 3 * QB])

        phase.close()

        act = tmp("act", [P, 2, FC, P])
        dot = tmp("dot", [P, 2, EXPERTS])
        top = tmp("top", [P, 2, RH, TOPK])
        tix = tmp("tix", [P, 2, RH, TOPK], u32)
        tixf = tmp("tixf", [P, RH, TOPK])
        tiy = tmp("tiy", [P, RH, TOPK], fp16)
        cand = tmp("cand", [P, RH, TOPK, TOPK])
        cand2 = tmp("cand2", [P, RH, TOPK, TOPK])
        best = tmp("best", [P, RH, TOPK])
        chosen = tmp("chosen", [P, RH, TOPK, TOPK])
        count = tmp("count", [P, RH, TOPK])
        epx = tmp("epx", [P, RH * (EX + NKEY + TOPK * TOPK)])
        zs = tmp("zs", [P, RH])
        rz = tmp("rz", [P, RH])
        exn = tmp("exn", [P, RH, EX])
        pc = tmp("pc", [P, RH, TOPK * TOPK])
        pcz = tmp("pcz", [P, RH, TOPK * TOPK])
        over = tmp("over", [P, RH, TOPK])
        chov = tmp("chov", [P, RH, TOPK, TOPK])
        wsil = tmp("wsil", [P, RH * TOPK * TOPK])
        wlast = tmp("wlast", [P, 1])
        ohx = tmp("ohx", [P, RH, EX, TOPK])
        dif = tmp("dif", [P, RH, NKEY, TOPK], fp16)
        nr = tmp("nr", [P, RH, NKEY + EX], fp16)
        nrT = tmp("nrT", [NKEY + EX, RH, P], fp16)
        oTs = tmp("oTs", [P, PAIRS, P])
        pxy = tmp("pxy", [P, RH, EX, NKEY])
        gsil = tmp("gsil", [P, 2, EX, NKEY])
        wh = tmp("wh", [P, 2, EXPERTS])
        wsum = tmp("wsum", [P, EXPERTS])
        wT = tmp("wT", [P, EC, P])

        phase.close()

        psum = ctx.enter_context(nc.psum_tensor("psum", [P, 8 * 512], fp32))
        bank = [psum[:, i * 512:(i + 1) * 512] for i in range(8)]

        ld_pat = [sem(f"ld_pat{g}") for g in range(GROUPS)]
        ld_rows = [sem(f"ld_rows{k}") for k in range(2)]
        ld_tok, ld_sel, ld_attn, ld_out, ld_misc, ld_ffn, ld_txt, st_out = map(sem, (
            "ld_tok", "ld_sel", "ld_attn", "ld_out", "ld_misc", "ld_ffn", "ld_txt", "st_out"))
        c_ident, c_pool, c_spread, c_bias, c_qks, c_null, c_nullT, c_nullk, c_simp, c_simW = map(sem, (
            "c_ident", "c_pool", "c_spread", "c_bias", "c_qks", "c_null", "c_nullT", "c_nullk", "c_simp", "c_simW"))
        p_stats, p_rstd, p_norm, t_tr, t_pT, t_mm, t_bias, t_stats, t_rstd, t_out = map(sem, (
            "p_stats", "p_rstd", "p_norm", "t_tr", "t_pT", "t_mm", "t_bias", "t_stats", "t_rstd", "t_out"))
        g_stats, g_rstd, g_norm, g_xhat, g_tr, g_T, g_slot, g_slotv = map(sem, (
            "g_stats", "g_rstd", "g_norm", "g_xhat", "g_tr", "g_T", "g_slot", "g_slotv"))
        a_qk, a_raw, a_v, a_sq, a_ss, a_rn, a_qkn, a_trq, a_trk, a_bias, a_qT, a_kT, a_nk, a_V, a_nv = map(sem, (
            "a_qk", "a_raw", "a_v", "a_sq", "a_ss", "a_rn", "a_qkn", "a_trq", "a_trk", "a_bias", "a_qT", "a_kT", "a_nk",
            "a_V", "a_nv"))
        a_sc, a_min, a_pr, a_trp, a_pT, a_rec, a_nm, a_o, a_oT = map(sem, (
            "a_sc", "a_min", "a_pr", "a_trp", "a_pT", "a_rec", "a_nm", "a_o", "a_oT"))
        f_stats, f_rstd, f_norm, f_trf, f_fT, f_simp, f_sim, f_up, f_act, f_dotp, f_dot = \
            map(sem, ("f_stats", "f_rstd", "f_norm", "f_trf", "f_fT", "f_simp",
                      "f_sim", "f_up", "f_act", "f_dotp", "f_dot"))
        f_sel, f_arg, f_exn, f_pcz, f_exp, f_px, f_gate, f_sil, f_wh, f_sum, f_last, f_wsil, f_trw, f_wT, f_y, \
            f_res, f_in, f_yo, f_hid, f_nr, f_trn, f_nrT, f_dif, f_tix, f_cnt, f_ohx, f_gate3 = \
            map(sem, ("f_sel", "f_arg", "f_exn", "f_pcz", "f_exp", "f_px", "f_gate", "f_sil", "f_wh", "f_sum", "f_last",
                      "f_wsil", "f_trw", "f_wT", "f_y", "f_res", "f_in", "f_yo", "f_hid", "f_nr", "f_trn", "f_nrT",
                      "f_dif", "f_tix", "f_cnt", "f_ohx", "f_gate3"))

        passed = {"dve": sem("passed_dve"), "pool": sem("passed_pool")}

        def wait_alone(engine, semaphore, value, name):
            engine.wait_ge(semaphore, value)
            engine.sem_inc(passed[name])

        def steps(engine, step):
            step(-1, 1, False, True, False, False)
            step(0, 0, True, True, True, False)
            with engine.Fori(0, TILES // 2 - 2) as tt:
                for k in range(1, 3):
                    step(tt * 2 + k, k % 2, True, True, True, True)
            step(TILES - 3, 1, True, True, True, True)
            step(TILES - 2, 0, False, True, True, True)
            step(TILES - 1, 1, False, False, True, True)
            step(TILES, 0, False, False, False, True)

        block = ctx.enter_context(nc.Block())

        @block.sync
        def _(sp):
            for g in range(GROUPS):
                sp.dma_start(pat[:, g, :], patches[g * P:(g + 1) * P, :]).then_inc(ld_pat[g], 16)
                if g == 0:
                    sp.dma_start(ln1g_sb[:], ln1_g).then_inc(ld_rows[0], 16)
                    sp.dma_start(ln1b_sb[:], ln1_b).then_inc(ld_rows[0], 16)
                    sp.dma_start(tokW_sb[:], tokW.rearrange("(c p) n -> p c n", p=P)).then_inc(ld_tok, 16)
            for k, row in enumerate((tok_b, ln2_g, ln2_b)):
                sp.dma_start(rows_sb[:, k, :], row).then_inc(ld_rows[1], 16)
            for g in range(GROUPS):
                sp.dma_start(hid[NPATCH:P, TPG * g, :], txt[2 * g, 0:NPATCH, :]).then_inc(ld_txt, 16)
                sp.dma_start(hid[0:NPATCH, TPG * g + 1, :], txt[2 * g, NPATCH:TXT, :]).then_inc(ld_txt, 16)
                sp.dma_start(hid[:, TPG * g + 2, :], txt[2 * g + 1, :, :]).then_inc(ld_txt, 16)
            sp.dma_start(Wr_sb, Wr.rearrange("(c p) n -> p c n", p=P)).then_inc(ld_sel, 16)
            sp.wait_ge(c_pool, 1)
            sp.dma_start(keyB[0:RN, :, 0:NKEY], keysT[0:RN]).then_inc(ld_sel, 16)
            sp.dma_start(keyB[RN:P, :, NKEY:P], keysT[RN:P]).then_inc(ld_sel, 16)
            for dst, src in ((qk_raw[:, 0:1], q_scale), (qk_raw[:, 1:2], k_scale),
                             (nullk[:].rearrange("r a d -> r (a d)"), null_k),
                             (nullv[QB:QB + NULL, :], null_v), (ng_sb[:], norm_g), (nb_sb[:], norm_b)):
                sp.dma_start(dst, src).then_inc(ld_misc, 16)
            for dst, src, done in ((Wq_sb, Wq, ld_attn), (Wkv_sb, Wkv, ld_attn), (Wout_sb, Wout, ld_out)):
                sp.dma_start(dst[:], src.rearrange("(c p) n -> p c n", p=P)).then_inc(done, 16)
            for dst, src in ((Wup_sb, WupT), (down_sb, downT), (Wdn_sb, WdownT),
                             (up_sb, upE)):
                sp.dma_start(dst[:], src.rearrange("(c p) n -> p c n", p=P)).then_inc(ld_ffn, 16)

            def store(t):
                sp.wait_ge(f_res, t + 1)
                sp.dma_start(out[bass.ds(t, 1)].rearrange("a p d -> p (a d)"),
                             hid[:, bass.ds(t, 1), :].rearrange("p a d -> p (a d)")).then_inc(st_out, 16)

            def attended(t):
                sp.dma_start(oTs[:], oT[:, :, bass.ds(t * P, P)]).then_inc(f_in, 16)

            sp.wait_ge(a_oT, GROUPS * PAIRS + 1)
            sp.wait_ge(f_yo, 3)
            attended(3)
            with sp.Fori(0, TILES - 5) as t:
                sp.wait_ge(f_yo, t + 4)
                attended(t + 4)
            with sp.Fori(0, TILES) as t:
                store(t)
            sp.wait_ge(st_out, 16 * TILES)

        @block.gpsimd
        def _(pool):
            nc.gpsimd.memset(keyB, 0.0).then_inc(c_pool, 1)
            nc.gpsimd.memset(ident[:], 0.0).then_inc(c_pool, 1)
            nc.gpsimd.memset(half[:], -0.5).then_inc(c_pool, 1)
            nc.gpsimd.memset(spread[:], 0.0).then_inc(c_pool, 1)
            nc.gpsimd.memset(ident16[:], 0.0).then_inc(c_pool, 1)
            pool.wait_ge(c_pool, 5)
            nc.gpsimd.affine_select(out=ident[:], in_=ident[:], compare_op=ALU.not_equal, fill=1.0, base=0,
                                    pattern=[[-1, P]], channel_multiplier=1).then_inc(c_ident, 1)
            nc.gpsimd.affine_select(out=ident16[:], in_=ident16[:], compare_op=ALU.not_equal, fill=1.0, base=0,
                                    pattern=[[-1, P]], channel_multiplier=1).then_inc(c_spread, 1)
            nc.gpsimd.affine_select(out=spread[0:NKEY], in_=spread[0:NKEY], compare_op=ALU.not_equal, fill=-1.0,
                                    base=0, pattern=[[0, EX], [-1, NKEY]], channel_multiplier=1).then_inc(c_spread, 1)
            pool.wait_ge(c_spread, 2)
            nc.gpsimd.affine_select(out=spread[NKEY:], in_=spread[NKEY:], compare_op=ALU.not_equal, fill=1.0,
                                    base=0, pattern=[[-1, EX], [0, NKEY]], channel_multiplier=1).then_inc(c_spread, 1)
            pool.wait_ge(c_spread, 3)

            pieces = ((0, QB, 0), (KA, QB, QB), (2 * KA, QB, 0))
            for at, n, base in pieces:
                nc.gpsimd.iota(dist[:, at:at + n], pattern=[[-1, n]], base=base, channel_multiplier=1,
                               allow_small_or_imprecise_dtypes=True).then_inc(c_pool, 1)
            for at, base in ((QB, NULL), (KA + QB, QB + NULL)):
                nc.gpsimd.iota(dist[:, at:at + NULL], pattern=[[-1, NULL]], base=base, channel_multiplier=1,
                               allow_small_or_imprecise_dtypes=True).then_inc(c_pool, 1)
            pool.wait_ge(c_pool, 10)
            for at in (0, 2 * KA):
                nc.gpsimd.affine_select(out=dist[:, at:at + QB], in_=dist[:, at:at + QB], compare_op=ALU.is_ge,
                                        fill=BIG, base=0, pattern=[[-1, QB]], channel_multiplier=1).then_inc(c_pool, 1)
            pool.wait_ge(c_pool, 12)
            start = 2.0 ** -0.5
            for h in range(HEADS):
                nc.gpsimd.memset(slope[:, h:h + 1], start * start ** h).then_inc(c_bias, 1)
            nc.gpsimd.iota(iox[:], pattern=[[1, EX], [0, TOPK]], base=0, channel_multiplier=0,
                           allow_small_or_imprecise_dtypes=True).then_inc(c_pool, 1)
            nc.gpsimd.iota(ioy[:], pattern=[[32, NKEY], [1, TOPK]], base=1, channel_multiplier=0,
                           allow_small_or_imprecise_dtypes=True).then_inc(c_pool, 1)

            def rstd(var, dst, before, done, scale=1.0, eps=EPS):
                pool.wait_ge(*before)
                nc.gpsimd.tensor_scalar(dst, var, scale, eps, ALU.mult, ALU.add).then_inc(done[0], 1)
                pool.wait_ge(done[0], done[1])
                nc.gpsimd.tensor_tensor(dst, dst, half[:, 0:dst.shape[-1]], ALU.pow).then_inc(done[0], 1)

            for g in range(GROUPS):
                rstd(p_mv[:, g, 1:2], p_rs[:, g:g + 1], (p_stats, 3 * g + 3), (p_rstd, 2 * g + 1))
            def token_rstd(g):
                rstd(t_mv[:, g, 1:2], t_rs[:, g:g + 1], (t_stats, 2 * g + 2), (t_rstd, 2 * g + 1))
            def block_rstd(g):
                var, mean = (g_mv[:, g, :, k:k + 1].rearrange("p t a -> p (t a)") for k in (1, 0))
                rstd(var, g_rs[:, g], (g_stats, 6 * g + 6), (g_rstd, 6 * g + 1))
                rstd(var, g_rs2[:, g], (g_stats, 6 * g + 6), (g_rstd, 6 * g + 3), 1.0 + EPS, EPS * EPS)
                pool.wait_ge(g_rstd, 6 * g + 4)
                nc.gpsimd.tensor_tensor(g_mr[:, g], g_rs2[:, g], mean, ALU.mult).then_inc(g_rstd, 1)
                pool.wait_ge(g_rstd, 6 * g + 5)
                nc.gpsimd.tensor_scalar(g_mr[:, g], g_mr[:, g], -1.0, None, ALU.mult).then_inc(g_rstd, 1)
            for g in range(GROUPS + 1):
                if g < GROUPS:
                    token_rstd(g)
                if g > 0:
                    block_rstd(g - 1)
            pool.wait_ge(c_null, 2)
            nc.gpsimd.tensor_scalar(nullk_ss[:], nullk_ss[:], 1e-24, None, ALU.max).then_inc(c_null, 1)
            pool.wait_ge(c_null, 3)
            nc.gpsimd.tensor_tensor(nullk_ss[:], nullk_ss[:], half[0:2 * PAIRS, 0:2], ALU.pow).then_inc(c_null, 1)

            def inv_norms(n):
                wait_alone(pool, a_ss, n + 1, "pool")
                nc.gpsimd.tensor_scalar(rn[:], ss[:], 1e-24, None, ALU.max).then_inc(a_rn, 1)
                pool.wait_ge(a_rn, 2 * n + 1)
                nc.gpsimd.tensor_tensor(rn[:], rn[:], half[:, 0:4 * TPG], ALU.pow).then_inc(a_rn, 1)
                wait_alone(pool, a_rn, 2 * n + 2, "pool")

            def null_keys(n, m, s):
                for b in range(2):
                    nc.gpsimd.tensor_copy(kT[:, s, b, QB:KA],
                                          nullkT[:, bass.ds(m, 1), :].rearrange("p a n -> p (a n)")).then_inc(a_nk, 1)
                wait_alone(pool, a_nk, 2 * n + 2, "pool")

            def null_values(n, m, s):
                for b in range(2):
                    nc.gpsimd.tensor_copy(V[QB:KA, s, 2 * b, :], nullv[QB:KA, bass.ds(m * P, P)]).then_inc(a_nv, 1)
                wait_alone(pool, a_nv, 2 * n + 2, "pool")

            def pair_bias(n, m, hh):
                nc.gpsimd.tensor_tensor(pbias[:, hh, :], dist[:], slope[:, bass.ds(m * 2 + hh, 1)].broadcast_to([QB, SC]),
                                        ALU.mult).then_inc(a_bias, 1)

            pool.wait_ge(c_bias, HEADS)
            pool.wait_ge(ld_misc, 96)
            for hh in range(2):
                pair_bias(0, 0, hh)
            inv_norms(0)
            pool.wait_ge(c_nullT, 2)
            null_keys(0, 0, 0)
            null_values(0, 0, 0)
            inv_norms(1)

            def ffn_norm(t):
                wait_alone(pool, f_stats, 2 * t + 2, "pool")
                nc.gpsimd.tensor_scalar(frs[:], fmv[:, 1:2], EPS, None, ALU.add).then_inc(f_rstd, 1)
                pool.wait_ge(f_rstd, 2 * t + 1)
                nc.gpsimd.tensor_tensor(frs[:], frs[:], half[:, 0:1], ALU.pow).then_inc(f_rstd, 1)

            def pair(n, s, m1, norms):
                wait_alone(pool, a_min, 8 * n + 6, "pool")
                pair_bias(n + 1, m1, 0)
                null_keys(n + 1, m1, 1 - s)
                wait_alone(pool, a_min, 8 * n + 8, "pool")
                pair_bias(n + 1, m1, 1)
                if norms:
                    inv_norms(n + 2)
                wait_alone(pool, a_oT, n + 1, "pool")
                null_values(n + 1, m1, 1 - s)

            def group(n0, last):
                with pool.Fori(0, PAIRS // 2 - 1) as j:
                    for s in range(2):
                        pair(n0 + j * 2 + s, s, j * 2 + (s + 1), True)
                pair(n0 + (PAIRS - 2), 0, PAIRS - 1, not last)
                if not last:
                    pair(n0 + (PAIRS - 1), 1, 0, True)

            with pool.Fori(0, GROUPS - 1) as g:
                group(g * PAIRS, False)
            group((GROUPS - 1) * PAIRS, True)
            ffn_norm(0)
            ffn_norm(1)

            def probabilities(t, h):
                if not isinstance(t, int) or t > 0:
                    pool.wait_ge(f_sil, 4 * t + h - 3)
                nc.gpsimd.tensor_tensor(
                    pxy[:, h], exn[:, h, :].unsqueeze(2).broadcast_to([P, EX, NKEY]),
                    epx[:, RH * EX + h * NKEY:RH * EX + (h + 1) * NKEY].unsqueeze(1).broadcast_to([P, EX, NKEY]),
                    ALU.mult).then_inc(f_px, 1)

            def add_head(t, h):
                pool.wait_ge(f_wh, 4 * t + h + 1)
                if h >= 2:
                    pool.wait_ge(f_sum, 3 * t + h - 1)
                elif not isinstance(t, int) or t > 0:
                    pool.wait_ge(f_trw, t)
                a = wh[:, 0, :] if h == 1 else wsum[:]
                nc.gpsimd.tensor_tensor(wsum[:], a, wh[:, h % 2, :], ALU.add).then_inc(f_sum, 1)

            def last_gate(t, slot):
                pool.wait_ge(f_dot, 2 * t + 2)
                pool.wait_ge(f_px, 4 * t + 4)
                x = pxy[:, RH - 1].rearrange("p x y -> p (x y)")
                nc.gpsimd.tensor_tensor(x, dot[:, slot, :], x, ALU.mult).then_inc(f_gate3, 1)

            def counts(t):
                pool.wait_ge(f_ohx, 3 * t + 1)
                pool.wait_ge(f_cnt, 2 * t + 2)
                nc.gpsimd.tensor_tensor(ohx[:], ohx[:], count[:].unsqueeze(2).broadcast_to([P, RH, EX, TOPK]),
                                        ALU.mult).then_inc(f_ohx, 1)
                nc.gpsimd.tensor_tensor(chov[:], chosen[:], over[:].unsqueeze(3).broadcast_to([P, RH, TOPK, TOPK]),
                                        ALU.mult).then_inc(f_ohx, 1)

            def step(t, slot, a, b, c, d):
                if c:
                    last_gate(t, slot)
                if a:
                    ffn_norm(t + 2)
                if c:
                    add_head(t, 1)
                if b:
                    counts(t + 1)
                if c:
                    add_head(t, 2)
                if b:
                    pool.wait_ge(f_exn, t + 2)
                    probabilities(t + 1, 0)
                    probabilities(t + 1, 1)
                    probabilities(t + 1, 2)
                if c:
                    add_head(t, 3)
                if b:
                    nc.gpsimd.tensor_tensor(pcz[:], pc[:], rz[:].unsqueeze(2).broadcast_to([P, RH, TOPK * TOPK]),
                                            ALU.mult).then_inc(f_pcz, 1)
                    probabilities(t + 1, 3)

            steps(pool, step)

        @block.vector
        def _(dve):
            def patch_stats(g):
                dve.wait_ge(ld_pat[g], 16)
                for k in range(2):
                    nc.vector.bn_stats(p_st[:, g, k, :], pat[:, g, k * (PDIM // 2):(k + 1) * (PDIM // 2)]).then_inc(p_stats, 1)
                dve.wait_ge(p_stats, 3 * g + 2)
                nc.vector.bn_aggr(p_mv[:, g, :], p_st[:, g]).then_inc(p_stats, 1)

            def patch_norm(g):
                dve.wait_ge(p_rstd, 2 * g + 2)
                nc.vector.tensor_scalar(pat[:, g, :], pat[:, g, :], p_mv[:, g, 0:1], p_rs[:, g:g + 1], ALU.subtract,
                                        ALU.mult).then_inc(p_norm, 1)

            def token_stats(g):
                dve.wait_ge(t_mm, g + 1)
                nc.vector.tensor_tensor(tk[:, g, :], bank[6 + g % 2][:, 0:DIM], rows_sb[:, 0, :], ALU.add).then_inc(t_bias, 1)
                dve.wait_ge(t_bias, g + 1)
                nc.vector.bn_stats(t_st[:, g, :], tk[:, g, :]).then_inc(t_stats, 1)
                dve.wait_ge(t_stats, 2 * g + 1)
                nc.vector.bn_aggr(t_mv[:, g, :], t_st[:, g, :]).then_inc(t_stats, 1)

            def token_norm(g):
                x = tk[:, g, :]
                dve.wait_ge(t_rstd, 2 * g + 2)
                nc.vector.tensor_scalar(x, x, t_mv[:, g, 0:1], t_rs[:, g:g + 1], ALU.subtract, ALU.mult).then_inc(t_out, 1)
                dve.wait_ge(t_out, 4 * g + 1)
                nc.vector.tensor_tensor(x, x, rows_sb[:, 1, :], ALU.mult).then_inc(t_out, 1)
                dve.wait_ge(t_out, 4 * g + 2)
                for lo, tile in ((0, 0), (NPATCH, 1)):
                    nc.vector.tensor_tensor(hid[lo:lo + NPATCH, TPG * g + tile, :], tk[lo:lo + NPATCH, g, :],
                                            rows_sb[lo:lo + NPATCH, 2, :], ALU.add).then_inc(t_out, 1)
                dve.wait_ge(t_out, 4 * g + 4)
                for t in range(TPG):
                    nc.vector.bn_stats(g_st[:, g, t, :], hid[:, TPG * g + t, :]).then_inc(g_stats, 1)
                for t in range(TPG):
                    dve.wait_ge(g_stats, 6 * g + 1 + t)
                    nc.vector.bn_aggr(g_mv[:, g, t, :], g_st[:, g, t, :]).then_inc(g_stats, 1)

            def block_norm(g):
                dve.wait_ge(g_rstd, 6 * g + 2)
                if g >= 2:
                    dve.wait_ge(g_tr, 4 * (g - 2) + 2)
                for t in range(TPG):
                    nc.vector.tensor_scalar(anorm[:, g % 2, t, :],
                                            hid[:, TPG * g + t, :], g_mv[:, g, t, 0:1], g_rs[:, g, t:t + 1],
                                            ALU.subtract, ALU.mult).then_inc(g_norm, 1)

            def operands(g):
                for dst, src in ((aT, aT_all), (xnT, xnT_all)):
                    nc.vector.tensor_copy(dst[:], src[:, :, bass.ds(g * TOK, TOK)]).then_inc(g_slot, 1)

            def operand_v(g):
                nc.vector.tensor_copy(aTv[:], aT_all[:, :, bass.ds(g * TOK, TOK)]).then_inc(g_slotv, 1)

            for g in range(GROUPS + 1):
                if g < GROUPS:
                    patch_stats(g)
                if g > 0:
                    patch_norm(g - 1)
            dve.wait_ge(ld_rows[1], 16 * 3)
            dve.wait_ge(ld_txt, 16 * 3 * GROUPS)
            for g in range(GROUPS + 2):
                if g < GROUPS:
                    token_stats(g)
                if 0 < g <= GROUPS:
                    token_norm(g - 1)
                if g > 1:
                    block_norm(g - 2)
                if g == GROUPS:
                    dve.wait_ge(g_T, 4)
                    operands(0)
                    operand_v(0)
            dve.wait_ge(ld_misc, 96)
            nc.vector.tensor_tensor(qks[:], qk_raw[:, 0:1], qk_raw[:, 1:2], ALU.mult).then_inc(c_qks, 1)
            nc.vector.tensor_tensor(nullk_sq[:], nullk[:], nullk[:], ALU.mult).then_inc(c_null, 1)
            dve.wait_ge(c_qks, 1)
            nc.vector.tensor_scalar(qks[:], qks[:], -8.0, None, ALU.mult).then_inc(c_qks, 1)
            dve.wait_ge(c_null, 1)
            nc.vector.tensor_reduce(nullk_ss[:], nullk_sq[:], axis=AX.X, op=ALU.add).then_inc(c_null, 1)
            dve.wait_ge(c_null, 4)
            nc.vector.tensor_tensor(nullk[:], nullk[:], nullk_ss[:].unsqueeze(2).broadcast_to([2 * PAIRS, 2, DH]),
                                    ALU.mult).then_inc(c_nullk, 1)
            def qk_norms(n):
                dve.wait_ge(a_sq, n + 1)
                nc.vector.tensor_reduce(ss[:], sq.rearrange("p (a d) -> p a d", d=DH), axis=AX.X,
                                        op=ALU.add).then_inc(a_ss, 1)

            def qk_scale(n, s):
                dve.wait_ge(a_rn, 2 * n + 2)
                x = qk[:, s, :].rearrange("p (a d) -> p a d", d=DH)
                nc.vector.tensor_tensor(x, x, rn[:].unsqueeze(2).broadcast_to([P, 4 * TPG, DH]),
                                        ALU.mult).then_inc(a_qkn, 1)

            def row_min(n, u):
                b, hh = divmod(u, 2)
                if b == 0:
                    dve.wait_ge(a_bias, 2 * n + hh + 1)
                wait_alone(dve, a_sc, 4 * n + u + 1, "dve")
                for q, (lo, cnt) in enumerate(((0, KA), (KA, KEYS))):
                    col = (b * 2 + q) * 2 + hh
                    nc.vector.tensor_tensor_reduce(
                        out=S[:, u % 2, lo:lo + cnt], in0=bank[3 + u % 2][0:QB, lo:lo + cnt],
                        in1=pbias[:, hh, lo:lo + cnt],
                        scale=1.0, scalar=BIG, op0=ALU.add, op1=ALU.min,
                        accum_out=rowmin[:, col:col + 1]).then_inc(a_min, 1)

            def of_head(x, s, u):
                b, hh = divmod(u, 2)
                return x[:, s, 4 * b:4 * b + 4].rearrange("p (q h) -> p q h", h=2)[:, :, hh:hh + 1]

            def probs_copy(n, u):
                dve.wait_ge(a_trp, 4 * n + u + 1)
                nc.vector.tensor_copy(pTs[:, u % 2, 0:2 * QB], bank[5 + u % 2][0:KA, 0:2 * QB]).then_inc(a_pT, 1)
                nc.vector.tensor_copy(pTs[0:QB, u % 2, 2 * QB:3 * QB],
                                      bank[5 + u % 2][0:QB, 2 * QB:3 * QB]).then_inc(a_pT, 1)

            def divide(n, u, s):
                b, hh = divmod(u, 2)
                dve.wait_ge(a_pr, 8 * n + 2 * u + 2)
                nc.vector.reciprocal(of_head(rrec, s, u), of_head(rowsum, s, u)).then_inc(a_rec, 1)
                dve.wait_ge(a_rec, 4 * n + u + 1)
                for q, (lo, cnt) in enumerate(((0, KA), (KA, KEYS))):
                    col = (b * 2 + q) * 2 + hh
                    x = probs[:, u % 2, lo:lo + cnt]
                    nc.vector.tensor_scalar(x, x, rrec[:, s, col:col + 1], None, ALU.mult).then_inc(a_nm, 1)

            def ffn_hid(t, home=6):
                dve.wait_ge(f_yo, t + 1)
                x = hid[:, bass.ds(t, 1), :].rearrange("p a d -> p (a d)")
                nc.vector.tensor_tensor(x, x, bank[home][:, 0:DIM], ALU.add).then_inc(f_hid, 1)
                wait_alone(dve, f_hid, t + 1, "dve")
                nc.vector.bn_stats(fst[:], x).then_inc(f_stats, 1)
                wait_alone(dve, f_stats, 2 * t + 1, "dve")
                nc.vector.bn_aggr(fmv[:], fst[:]).then_inc(f_stats, 1)

            def ffn_norm(t):
                dve.wait_ge(f_rstd, 2 * t + 2)
                nc.vector.tensor_scalar(fn[:], hid[:, bass.ds(t, 1), :].rearrange("p a d -> p (a d)"), fmv[:, 0:1],
                                        frs[:], ALU.subtract, ALU.mult).then_inc(f_norm, 1)

            def pair(n, s, c1, c2, next_qk=None, next_v=None, tile=None):
                probs_copy(n, 1)
                row_min(n, 3)
                divide(n, 2, s)
                if next_qk is not None:
                    wait_alone(dve, a_qk, 2 * n + 6, "dve")
                    operands(next_qk)
                if c2:
                    qk_norms(n + 2)
                probs_copy(n, 2)
                if c1:
                    row_min(n + 1, 0)
                divide(n, 3, s)
                if next_v is not None:
                    wait_alone(dve, a_v, n + 2, "dve")
                    operand_v(next_v)
                probs_copy(n, 3)
                if c1:
                    row_min(n + 1, 1)
                    divide(n + 1, 0, 1 - s)
                if tile is not None:
                    ffn_hid(tile, 0)
                if c2:
                    qk_scale(n + 2, s)
                if c1:
                    probs_copy(n + 1, 0)
                    row_min(n + 1, 2)
                    divide(n + 1, 1, 1 - s)
                if tile is not None:
                    ffn_norm(tile)

            qk_norms(0)
            qk_scale(0, 0)
            qk_norms(1)
            dve.wait_ge(g_T, 4 * GROUPS)
            row_min(0, 0)
            row_min(0, 1)
            divide(0, 0, 0)
            qk_scale(1, 1)
            probs_copy(0, 0)
            row_min(0, 2)
            divide(0, 1, 0)

            def group(g, last):
                n0 = g * PAIRS
                with dve.Fori(0, PAIRS // 2 - 2) as j:
                    for s in range(2):
                        pair(n0 + j * 2 + s, s, True, True)
                pair(n0 + (PAIRS - 4), 0, True, True)
                pair(n0 + (PAIRS - 3), 1, True, True, next_qk=None if last else g + 1)
                pair(n0 + (PAIRS - 2), 0, True, not last, next_v=None if last else g + 1, tile=0 if last else None)
                pair(n0 + (PAIRS - 1), 1, not last, not last, tile=1 if last else None)

            with dve.Fori(0, GROUPS - 1) as g:
                group(g, False)
            group(GROUPS - 1, True)
            dve.wait_ge(a_oT, GROUPS * PAIRS + 1)

            def gates(t, slot, h):
                dve.wait_ge(f_px, 4 * t + h + 1)
                if h == 0:
                    dve.wait_ge(f_dot, 2 * t + 2)
                x = pxy[:, h].rearrange("p x y -> p (x y)")
                nc.vector.tensor_tensor(x, dot[:, slot, :], x, ALU.mult).then_inc(f_gate, 1)

            def weights(t, h):
                dve.wait_ge(f_sil, 4 * t + h + 1)
                dve.wait_ge(f_dif, 4 * t + h + 1)
                if h >= 2:
                    dve.wait_ge(f_sum, 3 * t + 1)
                nc.vector.scalar_tensor_tensor(
                    out=wh[:, h % 2, :], in0=psum[:, (h % 2) * EXPERTS:(h % 2 + 1) * EXPERTS], scalar=0.0,
                    in1=gsil[:, h % 2].rearrange("p x y -> p (x y)"), op0=ALU.is_ge, op1=ALU.mult).then_inc(f_wh, 1)

            def step(t, slot, a, b, c, d):
                done = [0]
                other = 1 - slot

                def sel(ins):
                    ins.then_inc(f_sel, 1)
                    done[0] += 1
                    return done[0]

                def after(k):
                    wait_alone(dve, f_sel, (t + 1) * SEL_LEN + k, "dve")

                nx, ny = RH * EX, RH * NKEY
                if b:
                    wait_alone(dve, f_sim, t + 2, "dve")
                    for p in range(2):
                        for h in range(RH):
                            k = sel(nc.vector.max(top[:, p, h, :], sim[:, other, p, h, :]))
                if c:
                    gates(t, slot, 0)
                    gates(t, slot, 1)
                    gates(t, slot, 2)
                if b:
                    after(k)
                    kc = sel(nc.vector.tensor_tensor(
                        cand[:], top[:, 0].unsqueeze(3).broadcast_to([P, RH, TOPK, TOPK]),
                        top[:, 1].unsqueeze(2).broadcast_to([P, RH, TOPK, TOPK]), ALU.add))
                    for p in range(2):
                        for h in range(RH):
                            ki = sel(nc.vector.max_index(tix[:, p, h, :], top[:, p, h, :], sim[:, other, p, h, :]))
                if d:
                    add_last(t - 1)
                if b:
                    after(ki)
                    nc.vector.tensor_copy(tixf[:], tix[:, 0]).then_inc(f_tix, 1)
                    ky = sel(nc.vector.tensor_scalar(tiy[:], tix[:, 1], 32.0, None, ALU.mult))
                if c:
                    weights(t, 0)
                if b:
                    after(kc)
                    for h in range(RH):
                        kb = sel(nc.vector.max(best[:, h, :], cand[:, h].rearrange("p a b -> p (a b)")))
                    if c:
                        dve.wait_ge(f_px, 4 * t + 4)
                    nc.vector.tensor_tensor(
                        epx[:, 0:nx].rearrange("p (h x) -> p h x", h=RH), sim[:, other, 0, :, 0:EX],
                        top[:, 0, :, 0:1].broadcast_to([P, RH, EX]), ALU.subtract).then_inc(f_arg, 1)
                    nc.vector.tensor_tensor(
                        epx[:, nx:nx + ny].rearrange("p (h y) -> p h y", h=RH), sim[:, other, 1],
                        top[:, 1, :, 0:1].broadcast_to([P, RH, NKEY]), ALU.subtract).then_inc(f_arg, 1)
                    after(kb)
                    for h in range(RH):
                        kr = sel(nc.vector.match_replace(out=cand2[:, h].rearrange("p a b -> p (a b)"),
                                                         in_to_replace=best[:, h, :],
                                                         in_values=cand[:, h].rearrange("p a b -> p (a b)"),
                                                         imm_value=-BIG))
                    nc.vector.tensor_tensor(
                        epx[:, nx + ny:].rearrange("p (h c) -> p h c", h=RH), cand[:].rearrange("p h a b -> p h (a b)"),
                        best[:, :, 0:1].broadcast_to([P, RH, TOPK * TOPK]), ALU.subtract).then_inc(f_arg, 1)
                if a:
                    ffn_hid(t + 2)
                if c:
                    weights(t, 1)
                    last_expert(t)
                if b:
                    after(kr)
                    kh = sel(nc.vector.tensor_tensor(chosen[:], cand[:], cand2[:], ALU.not_equal))
                    dve.wait_ge(f_tix, t + 2)
                    nc.vector.tensor_tensor(ohx[:], iox[:].unsqueeze(1).broadcast_to([P, RH, EX, TOPK]),
                                            tixf[:].unsqueeze(2).broadcast_to([P, RH, EX, TOPK]),
                                            ALU.is_equal).then_inc(f_ohx, 1)
                    nc.vector.tensor_scalar(over[:], tixf[:], float(EX), None, ALU.is_ge).then_inc(f_cnt, 1)
                    after(kh)
                    nc.vector.tensor_reduce(count[:], chosen[:], axis=AX.X, op=ALU.add).then_inc(f_cnt, 1)
                if a:
                    ffn_norm(t + 2)
                if d:
                    finish(t - 1)
                if c:
                    weights(t, 2)
                if b:
                    after(ky)
                    kd = sel(nc.vector.tensor_tensor(
                        dif[:], ioy[:].unsqueeze(1).broadcast_to([P, RH, NKEY, TOPK]),
                        tiy[:].unsqueeze(2).broadcast_to([P, RH, NKEY, TOPK]), ALU.subtract))
                    dve.wait_ge(f_exp, t + 2)
                    kp = sel(nc.vector.tensor_tensor(pc[:], epx[:, nx + ny:].rearrange("p (h c) -> p h c", h=RH),
                                                     chosen[:].rearrange("p h a b -> p h (a b)"), ALU.mult))
                if b:
                    after(kp)
                    kz = sel(nc.vector.tensor_reduce(zs[:], pc[:], axis=AX.X, op=ALU.add))
                    after(kz)
                    kz = sel(nc.vector.reciprocal(rz[:], zs[:]))
                    after(kz)
                    nc.vector.tensor_tensor(exn[:], epx[:, 0:nx].rearrange("p (h x) -> p h x", h=RH),
                                            rz[:].unsqueeze(2).broadcast_to([P, RH, EX]), ALU.mult).then_inc(f_exn, 1)
                if c:
                    weights(t, 3)
                if b:
                    dve.wait_ge(f_ohx, 3 * t + 5)
                    nc.vector.tensor_reduce(nr[:, :, NKEY:], ohx[:], axis=AX.X, op=ALU.max).then_inc(f_nr, 1)
                    nc.vector.tensor_reduce(nr[:, :, 0:NKEY], dif[:], axis=AX.X, op=ALU.min,
                                            apply_absolute_value=True).then_inc(f_nr, 1)
                    assert done[0] == SEL_LEN, done[0]
            def last_expert(t):
                wait_alone(dve, f_wsil, t + 1, "dve")
                wait_alone(dve, f_ohx, 3 * t + 3, "dve")
                if not isinstance(t, int) or t > 0:
                    wait_alone(dve, f_last, 2 * t, "dve")
                nc.vector.tensor_tensor_reduce(out=pc[:].rearrange("p h c -> p (h c)"), in0=wsil[:],
                                               in1=chov[:].rearrange("p h a b -> p (h a b)"),
                                               scale=1.0, scalar=0.0, op0=ALU.mult, op1=ALU.add,
                                               accum_out=wlast[:]).then_inc(f_last, 1)

            def add_last(t):
                dve.wait_ge(f_sum, 3 * t + 3)
                nc.vector.tensor_tensor(wsum[:, EXPERTS - 1:EXPERTS], wsum[:, EXPERTS - 1:EXPERTS], wlast[:],
                                        ALU.add).then_inc(f_last, 1)

            def finish(t):
                dve.wait_ge(f_y, t + 1)
                x = hid[:, bass.ds(t, 1), :].rearrange("p a d -> p (a d)")
                nc.vector.tensor_tensor(x, x, bank[7][:, 0:DIM], ALU.add).then_inc(f_res, 1)

            steps(dve, step)

        @block.scalar
        def _(ac):
            def raw(n, k, s):
                cnt = (4 * P, 2 * P)[k]
                ac.wait_ge(a_qk, 2 * n + k + 1)
                nc.scalar.copy(qk[:, s, 4 * P * k:4 * P * k + cnt], bank[k][:, 0:cnt]).then_inc(a_raw, 1)

            def squares(n, s):
                ac.wait_ge(a_raw, 2 * n + 2)
                nc.scalar.activation(sq, qk[:, s, :], ACT.Square).then_inc(a_sq, 1)

            def exps(n, u, s):
                ac.wait_ge(a_min, 8 * n + 2 * u + 2)
                b, hh = divmod(u, 2)
                for q, (lo, cnt) in enumerate(((0, KA), (KA, KEYS))):
                    col = (b * 2 + q) * 2 + hh
                    nc.scalar.activation(probs[:, u % 2, lo:lo + cnt], S[:, u % 2, lo:lo + cnt], ACT.Exp,
                                         bias=rowmin[:, col:col + 1], scale=-1.0,
                                         accum_out=rowsum[:, s, col:col + 1]).then_inc(a_pr, 1)

            def qk_copies(n, s):
                ac.wait_ge(a_trq, n + 1)
                nc.scalar.activation(qT[:, s, :], bank[0][:, 0:TOK], ACT.Copy, scale=qks[:]).then_inc(a_qT, 1)
                ac.wait_ge(a_trk, n + 1)
                src = bank[1][:, 0:TOK].rearrange("p (b n) -> p b n", b=2)
                nc.scalar.copy(kT[:, s, :, 0:QB], src[:, :, 0:QB]).then_inc(a_kT, 1)
                nc.scalar.copy(kT[:, s, :, KA:KEYS], src[:, :, QB:N]).then_inc(a_kT, 1)

            def v_copy(n, s):
                ac.wait_ge(a_v, n + 1)
                nc.scalar.copy(V[0:QB, s].rearrange("p c d -> p (c d)"), bank[2][0:QB, :]).then_inc(a_V, 1)

            def fT_copy(t, slot, home=6):
                ac.wait_ge(f_trf, t + 1)
                nc.scalar.copy(fT[:, slot].rearrange("p c n -> p (c n)"), bank[home][:, DIM:2 * DIM]).then_inc(f_fT, 1)

            def sim_copy(t, slot, home=5):
                ac.wait_ge(f_simp, t + 1)
                nc.scalar.copy(sim[:, slot].rearrange("p a h k -> p (a h k)"), bank[home][:]).then_inc(f_sim, 1)

            def pair(n, g, m, s, c1, c2, c3):
                exps(n, 3, s)
                if not c1:
                    fT_copy(0, 0, 0)
                    sim_copy(0, 0, 1)
                if c1:
                    v_copy(n + 1, 1 - s)
                    exps(n + 1, 0, 1 - s)
                if c3:
                    raw(n + 3, 0, 1 - s)
                if c1:
                    exps(n + 1, 1, 1 - s)
                if c3:
                    raw(n + 3, 1, 1 - s)
                if c1:
                    exps(n + 1, 2, 1 - s)
                ac.wait_ge(a_o, n + 1)
                dst = oT[:, bass.ds(m, 1), bass.ds(g * TOK, TOK)].rearrange("p a n -> p (a n)")
                nc.scalar.copy(dst, bank[7][:, 0:TOK]).then_inc(a_oT, 1)
                if c2:
                    qk_copies(n + 2, s)
                if c3:
                    squares(n + 3, 1 - s)

            ac.sem_inc(a_oT)

            def both_norms(g):
                ac.wait_ge(g_rstd, 6 * g + 6)
                if g >= 2:
                    ac.wait_ge(g_tr, 4 * (g - 2) + 4)
                for t in range(TPG):
                    nc.scalar.activation(xhat[:, g % 2, t, :], hid[:, TPG * g + t, :], ACT.Identity,
                                         bias=g_mr[:, g, t:t + 1], scale=g_rs2[:, g, t:t + 1]).then_inc(g_xhat, 1)

            def inputs_T(g):
                for c in range(DC):
                    ac.wait_ge(g_tr, g * 4 + c + 1)
                    nc.scalar.copy(aT_all[:, c, g * TOK:(g + 1) * TOK], bank[4 + c][:, 0:TOK]).then_inc(g_T, 1)
                for c in range(DC):
                    ac.wait_ge(g_tr, g * 4 + 2 + c + 1)
                    nc.scalar.activation(xnT_all[:, c, g * TOK:(g + 1) * TOK], bank[6 + c][:, 0:TOK], ACT.Identity,
                                         bias=nb_sb[:, c:c + 1], scale=ng_sb[:, c:c + 1]).then_inc(g_T, 1)

            ac.wait_ge(ld_rows[0], 16 * 2)
            for g in range(GROUPS):
                ac.wait_ge(t_tr, g + 1)
                if g >= 2:
                    ac.wait_ge(t_mm, g - 1)
                for c in range(PC):
                    nc.scalar.activation(pT[:, g % 2, c, :], bank[2 * (g % 2) + c // 4][:, (c % 4) * P:(c % 4 + 1) * P],
                                         ACT.Identity, bias=ln1b_sb[:, c:c + 1], scale=ln1g_sb[:, c:c + 1]).then_inc(t_pT, 1)
            ac.wait_ge(c_simp, 1)
            for c in range(DC):
                nc.scalar.copy(simW[:, c, :], bank[c][:]).then_inc(c_simW, 1)
            ac.wait_ge(ld_misc, 96)
            for g in range(GROUPS):
                both_norms(g)
                if g > 0:
                    inputs_T(g - 1)
            for k in range(2):
                raw(0, k, 0)
            squares(0, 0)
            ac.wait_ge(c_nullT, 1)
            nc.scalar.copy(nullkT[:].rearrange("p m n -> p (m n)"), bank[3][:, 0:2 * PAIRS]).then_inc(c_nullT, 1)
            v_copy(0, 0)
            inputs_T(GROUPS - 1)
            ac.wait_ge(c_qks, 2)
            for k in range(2):
                raw(1, k, 1)
            ac.wait_ge(a_ss, 1)
            squares(1, 1)
            qk_copies(0, 0)
            exps(0, 0, 0)
            exps(0, 1, 0)
            for k in range(2):
                raw(2, k, 0)
            exps(0, 2, 0)
            qk_copies(1, 1)
            ac.wait_ge(a_ss, 2)
            squares(2, 0)

            def group(g, last):
                n0 = g * PAIRS
                with ac.Fori(0, PAIRS // 2 - 2) as j:
                    for s in range(2):
                        pair(n0 + j * 2 + s, g, j * 2 + s, s, True, True, True)
                for m in range(PAIRS - 4, PAIRS):
                    c1, c2, c3 = (not last or m < PAIRS - k for k in range(1, 4))
                    pair(n0 + m, g, m, m % 2, c1, c2, c3)

            with ac.Fori(0, GROUPS - 1) as g:
                group(g, False)
            group(GROUPS - 1, True)
            fT_copy(1, 1, 0)
            sim_copy(1, 1, 1)

            def dot_copy(t, slot, k):
                ac.wait_ge(f_dotp, 2 * t + 2 - k)
                nc.scalar.copy(dot[:, slot, k * 512:(k + 1) * 512], bank[6 + k][:]).then_inc(f_dot, 1)

            def dense_silu(t, slot, k):
                ac.wait_ge(f_up, 2 * t + k + 1)
                nc.scalar.activation(act[:, slot, 4 * k:4 * k + 4, :].rearrange("p c n -> p (c n)"), bank[4 + k][:],
                                     ACT.Silu).then_inc(f_act, 1)

            def silu(t, h):
                if h < RH - 1:
                    ac.wait_ge(f_gate, 3 * t + h + 1)
                else:
                    ac.wait_ge(f_gate3, t + 1)
                if h >= 2:
                    ac.wait_ge(f_wh, 4 * t + h - 1)
                nc.scalar.activation(gsil[:, h % 2].rearrange("p x y -> p (x y)"),
                                     pxy[:, h].rearrange("p x y -> p (x y)"), ACT.Silu).then_inc(f_sil, 1)

            def w_copies(t):
                ac.wait_ge(f_trw, t + 1)
                for k in range(2):
                    nc.scalar.copy(wT[:, 4 * k:4 * k + 4, :].rearrange("p c n -> p (c n)"), bank[4 + k][:]).then_inc(f_wT, 1)

            def step(t, slot, a, b, c, d):
                other = 1 - slot
                if c:
                    silu(t, 0)
                    silu(t, 1)
                    silu(t, 2)
                    ac.wait_ge(f_pcz, t + 1)
                    ac.wait_ge(f_dot, 2 * t + 2)
                    nc.scalar.activation(wsil[:], pcz[:].rearrange("p h c -> p (h c)"), ACT.Silu,
                                         scale=dot[:, slot, EXPERTS - 1:EXPERTS]).then_inc(f_wsil, 1)
                if d:
                    w_copies(t - 1)
                if c:
                    silu(t, 3)
                if b:
                    ac.wait_ge(f_arg, 3 * t + 6)
                    nc.scalar.activation(epx[:], epx[:], ACT.Exp).then_inc(f_exp, 1)
                if a:
                    fT_copy(t + 2, slot)
                if b:
                    dense_silu(t + 1, other, 0)
                    dot_copy(t + 1, other, 1)
                if a:
                    sim_copy(t + 2, slot)
                if b:
                    dot_copy(t + 1, other, 0)
                    dense_silu(t + 1, other, 1)
                    ac.wait_ge(f_trn, t + 2)
                    nc.scalar.copy(nrT[:].rearrange("r h n -> r (h n)"),
                                   bank[7][0:NKEY + EX, 0:DIM].bitcast(fp16)).then_inc(f_nrT, 1)

            steps(ac, step)

        @block.tensor
        def _(pe):
            mm = nc.tensor.matmul
            pe.wait_ge(c_ident, 1)
            pe.wait_ge(ld_tok, 16)

            def patches_T(g):
                pe.wait_ge(p_norm, g + 1)
                if g >= 2:
                    pe.wait_ge(t_pT, PC * (g - 1))
                for c in range(PC):
                    last = nc.tensor.transpose(bank[2 * (g % 2) + c // 4][:, (c % 4) * P:(c % 4 + 1) * P],
                                               pat[:, g, c * P:(c + 1) * P], ident[:])
                last.then_inc(t_tr, 1)

            def tokens(g):
                pe.wait_ge(t_pT, PC * g + PC)
                if g >= 2:
                    pe.wait_ge(t_bias, g - 1)
                for c in range(PC):
                    last = mm(bank[6 + g % 2][:, 0:DIM], pT[:, g % 2, c, :], tokW_sb[:, c, :], start=(c == 0),
                              stop=(c == PC - 1))
                last.then_inc(t_mm, 1)

            for g in range(GROUPS + 1):
                if g < GROUPS:
                    patches_T(g)
                if g > 0:
                    tokens(g - 1)
            pe.wait_ge(ld_sel, 48)
            for c in range(DC):
                for j in range(RH):
                    last = mm(bank[c][:, j * P:(j + 1) * P], Wr_sb[:, j, c * P:(c + 1) * P], keyB[:, j, :],
                              start=True, stop=True)
            last.then_inc(c_simp, 1)

            def inputs_T(g):
                for k, (src, done) in enumerate(((anorm, g_norm), (xhat, g_xhat))):
                    pe.wait_ge(done, TPG * (g + 1))
                    if g > 0:
                        pe.wait_ge(g_T, 4 * (g - 1) + 2 * k + 2)
                    for c in range(DC):
                        for t in range(TPG):
                            last = nc.tensor.transpose(bank[4 + 2 * k + c][:, t * P:(t + 1) * P],
                                                       src[:, g % 2, t, c * P:(c + 1) * P], ident[:])
                        last.then_inc(g_tr, 1)

            pe.wait_ge(t_bias, GROUPS)
            for g in range(GROUPS - 1):
                inputs_T(g)

            def project_qk(n, m, tiles):
                for t in tiles:
                    for j, (lhs, w) in enumerate(((xnT, Wq_sb), (aT, Wkv_sb))):
                        for c in range(DC):
                            last = mm(bank[t // 2][:, ((t % 2) * 2 + j) * P:((t % 2) * 2 + j + 1) * P],
                                      lhs[:, c, t * P:(t + 1) * P], w[:, c, bass.ds(m * P, P)],
                                      start=(c == 0), stop=(c == DC - 1))
                    if t:
                        last.then_inc(a_qk, 1)

            def project_v(n, m, blocks):
                for b in blocks:
                    for c in range(DC):
                        last = mm(bank[2][0:QB, b * P:(b + 1) * P], aTv[:, c, b * QB:(b + 1) * QB],
                                  Wkv_sb[:, c, bass.ds(m * P + INNER, P)], start=(c == 0), stop=(c == DC - 1))
                if b == 3:
                    last.then_inc(a_v, 1)

            def scores(n, u, s):
                b, hh = divmod(u, 2)
                lo = hh * DH
                for q, (at, cnt) in enumerate(((0, KA), (KA, KEYS))):
                    last = mm(bank[3 + u % 2][0:QB, at:at + cnt],
                              qT[lo:lo + DH, s, b * N + q * QB:b * N + (q + 1) * QB], kT[lo:lo + DH, s, b, 0:cnt],
                              start=True, stop=True)
                last.then_inc(a_sc, 1)

            def probs_T(n, u):
                pe.wait_ge(a_nm, 8 * n + 2 * u + 2)
                for k, (at, cnt) in enumerate(((0, KA), (KA, KA), (2 * KA, QB))):
                    last = nc.tensor.transpose(bank[5 + u % 2][0:cnt, k * QB:(k + 1) * QB],
                                               probs[:, u % 2, at:at + cnt], ident[0:QB, 0:QB])
                last.then_inc(a_trp, 1)

            def values(n, u, s):
                b, hh = divmod(u, 2)
                if u == 0:
                    pe.wait_ge(a_V, n + 1)
                    pe.wait_ge(a_nv, 2 * n + 2)
                    pe.wait_ge(a_oT, n + 1)
                pe.wait_ge(a_pT, 8 * n + 2 * u + 2)
                pp = pTs[:, u % 2]
                o = bank[7][hh * DH:(hh + 1) * DH, b * N:(b + 1) * N]
                mm(o, V[0:KA, s, 2 * b, hh * DH:(hh + 1) * DH], pp[:, 0:N], start=True, stop=False)
                last = mm(o[:, QB:N], V[0:QB, s, 2 * b + 1, hh * DH:(hh + 1) * DH], pp[0:QB, N:N + QB], start=False,
                          stop=True)
                if u == 3:
                    last.then_inc(a_o, 1)

            def qk_T(n, s):
                pe.wait_ge(a_raw, min_raw(n))
                pe.wait_ge(a_qkn, n + 1)
                for j, done in enumerate((a_trq, a_trk)):
                    for t in range(TPG):
                        last = nc.tensor.transpose(bank[j][:, t * P:(t + 1) * P],
                                                   qk[:, s, (2 * t + j) * P:(2 * t + j + 1) * P], ident[:])
                    last.then_inc(done, 1)

            def min_raw(n):
                return 2 * n + 4 if not isinstance(n, int) or n < GROUPS * PAIRS - 1 else 2 * n + 2

            def first_scores(n, u, s):
                if u == 0:
                    pe.wait_ge(a_qT, n + 1)
                    pe.wait_ge(a_kT, 2 * n + 2)
                    pe.wait_ge(a_nk, 2 * n + 2)
                scores(n, u, s)

            def out_projection(t, home=6):
                fixed = isinstance(t, int)
                if fixed and t == 0:
                    pe.wait_ge(ld_out, 16)
                if not fixed:
                    pe.wait_ge(f_in, 16 * (t - 2))
                for c in range(PAIRS):
                    lhs = oT[:, c, t * P:(t + 1) * P] if fixed else oTs[:, c, :]
                    last = mm(bank[home][:, 0:DIM], lhs, Wout_sb[:, c, :], start=(c == 0), stop=(c == PAIRS - 1))
                last.then_inc(f_yo, 1)

            def f_T(t, home=6):
                pe.wait_ge(f_norm, t + 1)
                for c in range(DC):
                    last = nc.tensor.transpose(bank[home][:, DIM + c * P:DIM + (c + 1) * P],
                                               fn[:, c * P:(c + 1) * P], ident[:])
                last.then_inc(f_trf, 1)

            def key_scores(t, slot, home=5):
                pe.wait_ge(f_fT, t + 1)
                for c in range(DC):
                    last = mm(bank[home][:], fT[:, slot, c, :], simW[:, c, :], start=(c == 0), stop=(c == DC - 1))
                last.then_inc(f_simp, 1)

            def pair(n, s, m1, m2, m3, slot=None, slotv=None, tile=None):
                probs_T(n, 1)
                scores(n, 3, s)
                values(n, 0, s)
                if m1 is not None:
                    project_v(n + 1, m1, (2, 3))
                probs_T(n, 2)
                if m1 is not None:
                    first_scores(n + 1, 0, 1 - s)
                values(n, 1, s)
                if tile == 1:
                    key_scores(0, 0, 1)
                if tile is not None:
                    out_projection(tile, 0)
                if m3 is not None:
                    if slot is not None:
                        pe.wait_ge(g_slot, slot)
                    project_qk(n + 3, m3, (0, 1))
                probs_T(n, 3)
                if m1 is not None:
                    first_scores(n + 1, 1, 1 - s)
                values(n, 2, s)
                if m3 is not None:
                    project_qk(n + 3, m3, (2,))
                if m1 is not None:
                    probs_T(n + 1, 0)
                    scores(n + 1, 2, 1 - s)
                values(n, 3, s)
                if m2 is not None:
                    qk_T(n + 2, s)
                    pe.wait_ge(a_V, n + 2)
                    if slotv is not None:
                        pe.wait_ge(g_slotv, slotv)
                    project_v(n + 2, m2, (0, 1))
                if tile is not None:
                    f_T(tile, 0)

            pe.wait_ge(c_simW, 2)
            pe.wait_ge(ld_attn, 32)
            pe.wait_ge(g_slot, 2)
            project_qk(0, 0, range(TPG))
            pe.wait_ge(c_nullk, 1)
            nc.tensor.transpose(bank[3][:, 0:2 * PAIRS], nullk[:].rearrange("r a d -> r (a d)"),
                                ident[0:2 * PAIRS, 0:2 * PAIRS]).then_inc(c_nullT, 1)
            pe.wait_ge(g_slotv, 1)
            project_v(0, 0, range(4))
            inputs_T(GROUPS - 1)
            pe.wait_ge(a_raw, 2)
            project_qk(1, 1, range(TPG))
            qk_T(0, 0)
            pe.wait_ge(g_T, 4 * GROUPS)
            pe.wait_ge(c_nullT, 2)
            first_scores(0, 0, 0)
            first_scores(0, 1, 0)
            project_qk(2, 2, range(TPG))
            probs_T(0, 0)
            scores(0, 2, 0)
            qk_T(1, 1)
            pe.wait_ge(a_V, 1)
            project_v(1, 1, (0, 1))

            def group(g, last):
                n0 = g * PAIRS
                with pe.Fori(0, PAIRS // 2 - 2) as j:
                    for s in range(2):
                        pair(n0 + j * 2 + s, s, j * 2 + (s + 1), j * 2 + (s + 2), j * 2 + (s + 3))
                for m in range(PAIRS - 4, PAIRS):
                    nxt = [None if last and m + k >= PAIRS else (m + k) % PAIRS for k in range(1, 4)]
                    pair(n0 + m, m % 2, *nxt, slot=2 * g + 4 if m == PAIRS - 3 and not last else None,
                         slotv=g + 2 if m == PAIRS - 2 and not last else None,
                         tile=m - (PAIRS - 2) if m >= PAIRS - 2 and last else None)

            with pe.Fori(0, GROUPS - 1) as g:
                group(g, False)
            group(GROUPS - 1, True)

            pe.wait_ge(f_sim, 1)
            key_scores(1, 1, 1)
            pe.wait_ge(ld_ffn, 16 * 4)
            pe.wait_ge(c_spread, 3)

            def expert_dots(t, slot, k):
                for c in range(DC):
                    last = mm(bank[6 + k][:], fT[:, slot, c, :], down_sb[:, c, k * 512:(k + 1) * 512],
                              start=(c == 0), stop=(c == DC - 1))
                last.then_inc(f_dotp, 1)

            def dense_up(t, slot, k):
                for j in range(4):
                    f = 4 * k + j
                    for c in range(DC):
                        last = mm(bank[4 + k][:, j * P:(j + 1) * P], Wup_sb[:, c, f * P:(f + 1) * P], fT[:, slot, c, :],
                                  start=(c == 0), stop=(c == DC - 1))
                last.then_inc(f_up, 1)

            def count_less_rank(t, h):
                for k in range(2):
                    last = mm(bank[2 * (h % 2) + k][:], nrT[:, h, :], spread[:, k * 512:(k + 1) * 512], start=True,
                              stop=True)
                last.then_inc(f_dif, 1)

            def down(slot, chunks):
                for k in chunks:
                    mm(bank[7][:, 0:DIM], act[:, slot, k, :], Wdn_sb[:, k, :], start=(k == 0), stop=False)

            def step(t, slot, a, b, c, d):
                other = 1 - slot
                if a:
                    if c:
                        pe.wait_ge(f_dot, 2 * t + 2)
                    out_projection(t + 2)
                if c:
                    pe.wait_ge(f_nrT, t + 1)
                    if d:
                        pe.wait_ge(f_wh, 4 * t)
                    count_less_rank(t, 0)
                    count_less_rank(t, 1)
                if c:
                    pe.wait_ge(f_act, 2 * t + 2)
                if d:
                    if not c:
                        pe.wait_ge(f_res, t - 1)
                    down(other, range(FC // 2))
                    pe.wait_ge(f_last, 2 * t)
                    for e in range(EC):
                        last = nc.tensor.transpose(bank[4 + e // 4][:, (e % 4) * P:(e % 4 + 1) * P],
                                                   wsum[:, e * P:(e + 1) * P], ident[:])
                    last.then_inc(f_trw, 1)
                    down(other, range(FC // 2, FC))
                if c:
                    pe.wait_ge(f_wh, 4 * t + 1)
                    count_less_rank(t, 2)
                if d:
                    pe.wait_ge(f_wT, 2 * t)
                    for e in range(EC):
                        last = mm(bank[7][:, 0:DIM], wT[:, e, :], up_sb[:, e, :], start=False, stop=(e == EC - 1))
                    last.then_inc(f_y, 1)
                if b:
                    dense_up(t + 1, other, 0)
                if c:
                    pe.wait_ge(f_wh, 4 * t + 2)
                    count_less_rank(t, 3)
                if a:
                    f_T(t + 2)
                if b:
                    if d:
                        pe.wait_ge(f_res, t)
                    expert_dots(t + 1, other, 1)
                if a:
                    key_scores(t + 2, slot)
                if b:
                    expert_dots(t + 1, other, 0)
                    if a:
                        pe.wait_ge(f_sim, t + 3)
                    dense_up(t + 1, other, 1)
                    pe.wait_ge(f_nr, 2 * t + 4)
                    pe.wait_ge(f_dot, 2 * t + 4)
                    for h in range(RH):
                        last = nc.tensor.transpose(bank[7][0:NKEY + EX, 0:DIM].bitcast(fp16)[:, h * P:(h + 1) * P],
                                                   nr[:, h, :], ident16[:])
                    last.then_inc(f_trn, 1)

            steps(pe, step)


_INS = ("patches", "txt", "ln1_g", "ln1_b", "tokW", "tok_b", "ln2_g", "ln2_b", "norm_g", "norm_b", "Wq", "Wkv",
        "q_scale", "k_scale", "null_k", "null_v", "Wout", "WupT", "WdownT", "Wr", "keysT", "downT", "upE")


def kernel(**inputs):
    import numpy as np
    import concourse.bacc as bacc
    from concourse.bass_utils import run_bass_kernel_spmd

    a = {k: np.asarray(v) for k, v in inputs.items()}

    def rows(v):
        return np.broadcast_to(v[None, :], (P, v.shape[0]))

    def by_feature(v):
        return v.reshape(-1, P).T

    null = a["L0_attn_null_kv"].reshape(PAIRS, 2, NULL, 2, DH)
    laid = {
        "patches": a["x"].reshape(B, CH, GRID, PATCH, GRID, PATCH).transpose(0, 2, 4, 3, 5, 1).reshape(B * NPATCH, PDIM),
        "txt": a["txt"],
        "ln1_g": by_feature(a["L0_tok_ln1_g"]), "ln1_b": by_feature(a["L0_tok_ln1_b"]), "tokW": a["L0_tok_W"],
        "tok_b": rows(a["L0_tok_b"]), "ln2_g": rows(a["L0_tok_ln2_g"]), "ln2_b": rows(a["L0_tok_ln2_b"]),
        "norm_g": by_feature(a["L0_attn_norm_g"]), "norm_b": by_feature(a["L0_attn_norm_b"]),
        "Wq": a["L0_attn_Wq"], "Wkv": a["L0_attn_Wkv"],
        "q_scale": np.tile(a["L0_attn_q_scale"], 2)[:, None], "k_scale": np.tile(a["L0_attn_k_scale"], 2)[:, None],
        "null_k": null[:, :, :, 0].transpose(0, 2, 1, 3).reshape(PAIRS * NULL, 2 * DH),
        "null_v": null[:, :, :, 1].transpose(2, 0, 1, 3).reshape(NULL, INNER),
        "Wout": a["L0_attn_Wout"], "WupT": a["L0_ffn_W_up"].T, "WdownT": a["L0_ffn_W_down"].T,
        "Wr": a["L0_ffn_W_q"],
        "keysT": a["L0_ffn_keys"].reshape(2, 2, NKEY, 2, RN).transpose(1, 4, 3, 0, 2).reshape(2 * RN, RH, NKEY),
        "downT": a["L0_ffn_down_embed"].T, "upE": a["L0_ffn_up_embed"],
    }
    nc = bacc.Bacc("TRN2", target_bir_lowering=False, num_devices=1)
    arrays, args = {}, []
    for name in _INS:
        arrays[name] = np.ascontiguousarray(laid[name])
        args.append(nc.dram_tensor(name, arrays[name].shape, mybir.dt.from_np(arrays[name].dtype),
                                   kind="ExternalInput").ap())
    out = nc.dram_tensor("out", (B, N, DIM), mybir.dt.float32, kind="ExternalOutput").ap()
    build_program(nc, *args, out.rearrange("b n d -> (b n) d").rearrange("(t p) d -> t p d", p=P))
    r = run_bass_kernel_spmd(nc, [arrays], core_ids=[0])
    return r.results[0]["out"]
```
